# Optimizing a Trainium2 kernel written in Bass

```python
import numpy as np
import jax
import jax.numpy as jnp

def _softmax(x, axis=-1):
    return jax.nn.softmax(x, axis=axis)

def _gelu(x):
    return jax.nn.gelu(x, approximate=True)

def _silu(x):
    return jax.nn.silu(x)

def _sigmoid(x):
    return jax.nn.sigmoid(x)

def _layernorm(x, axis=-1, eps=1e-05):
    m = jnp.mean(x, axis=axis, keepdims=True)
    v = jnp.var(x, axis=axis, keepdims=True)
    return (x - m) / jnp.sqrt(v + eps)

def _scatter_add(tgt, idx, src, axis=0):
    return tgt.at[idx].add(src)

def _segment_sum(src, seg, n):
    return jax.ops.segment_sum(src, seg, n)
kernel_name = 'mk_decoder_preln_d1_seqx_r8_19141d'

def setup_inputs(seed: int=0):
    np.random.seed(seed)
    _w = jnp.asarray

    def _rec_inputs():
        import jax
        import jax.numpy as jnp
        _rk = jax.random.key(seed)
        x = 2.818e-05 + 1 * jax.random.normal(jax.random.fold_in(_rk, 1), (8, 256, 128), jnp.float32)
        _lenS = 256 - jax.random.randint(jax.random.fold_in(_rk, 7), (8,), 0, max(1, 256 // 4) + 1, jnp.int32)
        _lenS2 = 256 - jax.random.randint(jax.random.fold_in(_rk, 8), (8,), 0, max(1, 256 // 4) + 1, jnp.int32)
        _ctx_2048P = jax.random.normal(jax.random.fold_in(_rk, 11), (8, 16, 256), jnp.float32)
        _ctx_2048c = jax.random.dirichlet(jax.random.fold_in(_rk, 511), 0.3 * jnp.ones((16,), jnp.float32), (8, 256))
        _ctx_2048t = jnp.einsum('bsk,bkd->bsd', _ctx_2048c, _ctx_2048P)
        _ctx_2048t = _ctx_2048t * jax.lax.rsqrt(jnp.mean(jnp.square(_ctx_2048t)) + 1e-12) * 0.953939
        ctx_2048 = -0.000125008 + 0.999885 * (_ctx_2048t + 0.3 * jax.random.normal(jax.random.fold_in(_rk, 611), (8, 256, 256), jnp.float32))
        _validS = jnp.arange(256)[None, :] < _lenS[:, None]
        _validS2 = jnp.arange(256)[None, :] < _lenS2[:, None]
        _causal = jnp.tril(jnp.ones((256, 256), dtype=bool))
        mask_BxS2_fk1 = jnp.where(jnp.broadcast_to(_validS2[:, :], (8, 256)), 1.0, 0.0).astype(jnp.float32)
        return (x, ctx_2048, mask_BxS2_fk1)
    x, ctx_2048, mask_BxS2_fk1 = _rec_inputs()

    def _L0_attn_setup():
        import jax, jax.numpy as jnp
        import numpy as np
        B, T, D_MODEL, STATE = (4, 512, 128, 32)
        LN_EPS = 1e-05

        def _layernorm(x, w, b):
            mu = jnp.mean(x, axis=-1, keepdims=True)
            var = jnp.mean(jnp.square(x - mu), axis=-1, keepdims=True)
            return (x - mu) * jax.lax.rsqrt(var + LN_EPS) * w + b
        key = jax.random.key(seed)
        ks = jax.random.split(key, 8)
        x = jax.random.normal(ks[0], (B, T, D_MODEL), dtype=jnp.float32)
        bound_d = 1.0 / np.sqrt(D_MODEL)
        bound_n = 1.0 / np.sqrt(STATE)
        Wa_w = jax.random.normal(ks[1], (STATE, D_MODEL), dtype=jnp.float32) * 0.02
        Wa_b = jnp.zeros((STATE,), dtype=jnp.float32)
        WB_w = jax.random.normal(ks[2], (STATE, D_MODEL), dtype=jnp.float32) * 0.02
        WB_b = jax.random.uniform(ks[3], (STATE,), jnp.float32, -bound_d, bound_d)
        WC_w = jax.random.normal(ks[4], (D_MODEL, STATE), dtype=jnp.float32) * 0.02
        WC_b = jax.random.uniform(ks[5], (D_MODEL,), jnp.float32, -bound_n, bound_n)
        log_gamma = jnp.asarray(0.0, dtype=jnp.float32)
        D_skip = jax.random.normal(ks[6], (D_MODEL,), dtype=jnp.float32) * 0.01
        ln_w = jnp.ones((D_MODEL,), dtype=jnp.float32)
        ln_b = jnp.zeros((D_MODEL,), dtype=jnp.float32)
        return {'x': x, 'Wa_w': Wa_w, 'Wa_b': Wa_b, 'log_gamma': log_gamma, 'WB_w': WB_w, 'WB_b': WB_b, 'WC_w': WC_w, 'WC_b': WC_b, 'D_skip': D_skip, 'ln_w': ln_w, 'ln_b': ln_b}
    _L0_attn_all = _L0_attn_setup()
    _L0_attn_in = {k: v for k, v in _L0_attn_all.items() if k in ('Wa_w', 'Wa_b', 'log_gamma', 'WB_w', 'WB_b', 'WC_w', 'WC_b', 'D_skip', 'ln_w', 'ln_b')}
    del _L0_attn_all

    def _L0_xattn_setup():
        import jax, jax.numpy as jnp
        import numpy as np
        B, S, T = (32, 64, 64)
        SRC_SIZE, TGT_SIZE, OUT_SIZE, NUM_HEAD = (256, 128, 128, 8)
        HEAD_DIM = OUT_SIZE // NUM_HEAD
        key = jax.random.key(seed)
        ks = jax.random.split(key, 12)
        src = jax.random.normal(ks[0], (B, S, SRC_SIZE), dtype=jnp.float32)
        tgt = jax.random.normal(ks[1], (B, T, TGT_SIZE), dtype=jnp.float32)
        src_mask = (jax.random.uniform(ks[2], (B, S)) > 0.3).astype(jnp.float32)
        src_mask = src_mask.at[:, 0].set(1.0)
        tgt_mask = (jax.random.uniform(ks[3], (B, T)) > 0.3).astype(jnp.float32)
        tgt_mask = tgt_mask.at[:, 0].set(1.0)

        def lin(k, out_f, in_f):
            return jax.random.normal(k, (out_f, in_f), dtype=jnp.float32) / np.sqrt(in_f)
        W_src = lin(ks[4], 2 * OUT_SIZE, SRC_SIZE)
        b_src = jnp.zeros((2 * OUT_SIZE,), jnp.float32)
        W_tgt = lin(ks[5], OUT_SIZE, TGT_SIZE)
        b_tgt = jnp.zeros((OUT_SIZE,), jnp.float32)
        W_out = lin(ks[6], OUT_SIZE, OUT_SIZE + TGT_SIZE)
        b_out = jnp.zeros((OUT_SIZE,), jnp.float32)
        return {'src': src, 'tgt': tgt, 'src_mask': src_mask, 'tgt_mask': tgt_mask, 'W_src': W_src, 'b_src': b_src, 'W_tgt': W_tgt, 'b_tgt': b_tgt, 'W_out': W_out, 'b_out': b_out}
    _L0_xattn_all = _L0_xattn_setup()
    _L0_xattn_in = {k: v for k, v in _L0_xattn_all.items() if k in ('W_src', 'b_src', 'W_tgt', 'b_tgt', 'W_out', 'b_out')}
    del _L0_xattn_all

    def _L0_ffn_setup():
        import jax, jax.numpy as jnp
        import numpy as np
        DIM = 128
        DEPTH = 6
        HEADS = 16
        DIM_HEAD = 64
        WINDOW = 32
        INNER = HEADS * DIM_HEAD
        DIM_INNER = int(DIM * 4 * 2 / 3)
        QK_SCALE = 8.0

        def shift_tokens(t):
            a, s = jnp.split(t, 2, -1)
            s = jnp.pad(s, ((0, 0), (1, 0), (0, 0)))[:, :-1]
            return jnp.concatenate([a, s], -1)

        def l2norm(t):
            return t / jnp.maximum(jnp.linalg.norm(t, axis=-1, keepdims=True), 1e-12)

        def rotate_half(x):
            x1, x2 = jnp.split(x, 2, -1)
            return jnp.concatenate([-x2, x1], -1)

        def rotary_tables(n):
            half = jnp.arange(0, DIM_HEAD, 2, dtype=jnp.float32)
            inv_freq = 1.0 / 10000.0 ** (half / DIM_HEAD)
            t = jnp.arange(n, dtype=jnp.float32)
            freqs = t[:, None] * inv_freq[None, :]
            freqs = jnp.concatenate([freqs, freqs], -1)
            base_scale = (half + 0.4 * DIM_HEAD) / (1.4 * DIM_HEAD)
            power = (t - n // 2) / (WINDOW // 2)
            scale = base_scale[None, :] ** power[:, None]
            scale = jnp.concatenate([scale, scale], -1)
            return (freqs, scale)

        def local_attention(q, k, v):
            b, h, n, d = q.shape
            w = WINDOW
            nw = n // w
            bq = q.reshape(b, h, nw, w, d)
            bk = k.reshape(b, h, nw, w, d)
            bv = v.reshape(b, h, nw, w, d)

            def look(t):
                p = jnp.pad(t, ((0, 0), (0, 0), (1, 0), (0, 0), (0, 0)))
                return jnp.concatenate([p[:, :, :nw], p[:, :, 1:]], axis=3)
            bk2, bv2 = (look(bk), look(bv))
            seq = jnp.arange(n).reshape(nw, w)
            seq_p = jnp.pad(seq, ((1, 0), (0, 0)), constant_values=-1)
            jt = jnp.concatenate([seq_p[:nw], seq_p[1:]], axis=1)
            it = seq[:, :, None]
            jb = jt[:, None, :]
            mask = (it < jb) | (it > jb + w) | (jb == -1)
            sim = jnp.einsum('bhwie,bhwje->bhwij', bq, bk2) * QK_SCALE
            sim = jnp.where(mask, -jnp.finfo(sim.dtype).max, sim)
            attn = jax.nn.softmax(sim, -1)
            out = jnp.einsum('bhwij,bhwje->bhwie', attn, bv2)
            return out.reshape(b, h, n, d)

        def attn_layer(x, Wqkv, qs, ksc, Wo):
            b, n, _ = x.shape
            qkv = x @ Wqkv
            q, k, v = jnp.split(qkv, 3, -1)
            sh = lambda t: t.reshape(b, n, HEADS, DIM_HEAD).transpose(0, 2, 1, 3)
            q, k, v = (sh(q), sh(k), sh(v))
            q = l2norm(q) * qs
            k = l2norm(k) * ksc
            freqs, scale = rotary_tables(n)
            cos, sin = (jnp.cos(freqs), jnp.sin(freqs))
            q = q * cos * scale + rotate_half(q) * sin * scale
            inv = 1.0 / scale
            k = k * cos * inv + rotate_half(k) * sin * inv
            out = local_attention(q, k, v)
            out = out.transpose(0, 2, 1, 3).reshape(b, n, INNER)
            return out @ Wo

        def ffn_layer(x, g, bln, W1, b1, W2, b2):
            mu = x.mean(-1, keepdims=True)
            var = ((x - mu) ** 2).mean(-1, keepdims=True)
            xn = (x - mu) / jnp.sqrt(var + 1e-05) * g + bln
            hg = xn @ W1 + b1
            a, gate = jnp.split(hg, 2, -1)
            return a * jax.nn.gelu(gate, approximate=False) @ W2 + b2
        key = jax.random.key(seed)
        ks = jax.random.split(key, 8)
        B, N = (2, 256)
        init = lambda k, shape: jax.random.normal(k, shape, jnp.float32) * 0.02
        return {'x': jax.random.normal(ks[0], (B, N, DIM), jnp.float32), 'Wqkv': init(ks[1], (DEPTH, DIM, 3 * INNER)), 'q_scale': jnp.ones((DEPTH, DIM_HEAD), jnp.float32), 'k_scale': jnp.ones((DEPTH, DIM_HEAD), jnp.float32), 'Wo': init(ks[2], (DEPTH, INNER, DIM)), 'ln_g': jnp.ones((DEPTH, DIM), jnp.float32), 'ln_b': jnp.zeros((DEPTH, DIM), jnp.float32), 'W1': init(ks[3], (DEPTH, DIM, 2 * DIM_INNER)), 'b1': jnp.zeros((DEPTH, 2 * DIM_INNER), jnp.float32), 'W2': init(ks[4], (DEPTH, DIM_INNER, DIM)), 'b2': jnp.zeros((DEPTH, DIM), jnp.float32)}
    _L0_ffn_all = _L0_ffn_setup()
    _L0_ffn_in = {k: v for k, v in _L0_ffn_all.items() if k in ('Wqkv', 'q_scale', 'k_scale', 'Wo', 'ln_g', 'ln_b', 'W1', 'b1', 'W2', 'b2')}
    del _L0_ffn_all
    return {'x': x, 'ctx_2048': ctx_2048, 'mask_BxS2_fk1': mask_BxS2_fk1, 'L0_attn_Wa_w': _L0_attn_in['Wa_w'], 'L0_attn_Wa_b': _L0_attn_in['Wa_b'], 'L0_attn_log_gamma': _L0_attn_in['log_gamma'], 'L0_attn_WB_w': _L0_attn_in['WB_w'], 'L0_attn_WB_b': _L0_attn_in['WB_b'], 'L0_attn_WC_w': _L0_attn_in['WC_w'], 'L0_attn_WC_b': _L0_attn_in['WC_b'], 'L0_attn_D_skip': _L0_attn_in['D_skip'], 'L0_attn_ln_w': _L0_attn_in['ln_w'], 'L0_attn_ln_b': _L0_attn_in['ln_b'], 'L0_xattn_W_src': _L0_xattn_in['W_src'], 'L0_xattn_b_src': _L0_xattn_in['b_src'], 'L0_xattn_W_tgt': _L0_xattn_in['W_tgt'], 'L0_xattn_b_tgt': _L0_xattn_in['b_tgt'], 'L0_xattn_W_out': _L0_xattn_in['W_out'], 'L0_xattn_b_out': _L0_xattn_in['b_out'], 'L0_ffn_Wqkv': _L0_ffn_in['Wqkv'], 'L0_ffn_q_scale': _L0_ffn_in['q_scale'], 'L0_ffn_k_scale': _L0_ffn_in['k_scale'], 'L0_ffn_Wo': _L0_ffn_in['Wo'], 'L0_ffn_ln_g': _L0_ffn_in['ln_g'], 'L0_ffn_ln_b': _L0_ffn_in['ln_b'], 'L0_ffn_W1': _L0_ffn_in['W1'], 'L0_ffn_b1': _L0_ffn_in['b1'], 'L0_ffn_W2': _L0_ffn_in['W2'], 'L0_ffn_b2': _L0_ffn_in['b2']}

def reference(x, ctx_2048, mask_BxS2_fk1, L0_attn_Wa_w, L0_attn_Wa_b, L0_attn_log_gamma, L0_attn_WB_w, L0_attn_WB_b, L0_attn_WC_w, L0_attn_WC_b, L0_attn_D_skip, L0_attn_ln_w, L0_attn_ln_b, L0_xattn_W_src, L0_xattn_b_src, L0_xattn_W_tgt, L0_xattn_b_tgt, L0_xattn_W_out, L0_xattn_b_out, L0_ffn_Wqkv, L0_ffn_q_scale, L0_ffn_k_scale, L0_ffn_Wo, L0_ffn_ln_g, L0_ffn_ln_b, L0_ffn_W1, L0_ffn_b1, L0_ffn_W2, L0_ffn_b2):
    import jax
    import jax.numpy as jnp

    def _L0_attn_ref(x, Wa_w, Wa_b, log_gamma, WB_w, WB_b, WC_w, WC_b, D_skip, ln_w, ln_b):
        import jax, jax.numpy as jnp
        import numpy as np
        B, T, D_MODEL, STATE = (4, 512, 128, 32)
        LN_EPS = 1e-05

        def _layernorm(x, w, b):
            mu = jnp.mean(x, axis=-1, keepdims=True)
            var = jnp.mean(jnp.square(x - mu), axis=-1, keepdims=True)
            return (x - mu) * jax.lax.rsqrt(var + LN_EPS) * w + b
        residual = x
        xn = _layernorm(x, ln_w, ln_b)
        gamma = jax.nn.sigmoid(log_gamma)
        a = gamma * jnp.tanh(jnp.einsum('btd,nd->btn', xn, Wa_w) + Wa_b)
        a_hat = jnp.fft.fft(a, axis=-1)
        mag = jnp.maximum(jnp.abs(a_hat), 1e-08)
        a_hat = a_hat * jax.nn.sigmoid(2.0 * (1.0 - mag))
        u = jnp.einsum('btd,nd->btn', xn, WB_w) + WB_b
        u_hat = jnp.fft.fft(u, axis=-1)

        def combine(c1, c2):
            a1, b1 = c1
            a2, b2 = c2
            return (a1 * a2, a2 * b1 + b2)
        _, h_hat = jax.lax.associative_scan(combine, (a_hat, u_hat), axis=1)
        h = jnp.real(jnp.fft.ifft(h_hat, axis=-1)).astype(x.dtype)
        y = jnp.einsum('btn,dn->btd', h, WC_w) + WC_b + D_skip * residual
        return y

    def _L0_xattn_ref(src, tgt, src_mask, tgt_mask, W_src, b_src, W_tgt, b_tgt, W_out, b_out):
        import jax, jax.numpy as jnp
        import numpy as np
        B, S, T = (32, 64, 64)
        SRC_SIZE, TGT_SIZE, OUT_SIZE, NUM_HEAD = (256, 128, 128, 8)
        HEAD_DIM = OUT_SIZE // NUM_HEAD
        b, s, _ = src.shape
        t = tgt.shape[1]
        src_trans = jnp.einsum('bsf,of->bso', src, W_src) + b_src
        tgt_trans = jnp.einsum('btf,of->bto', tgt, W_tgt) + b_tgt
        src_trans = src_trans * src_mask[:, :, None]
        tgt_trans = tgt_trans * tgt_mask[:, :, None]
        src_key, src_val = jnp.split(src_trans, 2, axis=2)
        k = src_key.reshape(b, s, NUM_HEAD, HEAD_DIM)
        v = src_val.reshape(b, s, NUM_HEAD, HEAD_DIM)
        q = tgt_trans.reshape(b, t, NUM_HEAD, HEAD_DIM)
        scores = jnp.einsum('bthd,bshd->bhts', q, k) / np.sqrt(HEAD_DIM)
        scores = jnp.where(src_mask[:, None, None, :] == 0, -jnp.inf, scores)
        attn = jax.nn.softmax(scores, axis=-1)
        tgt_update = jnp.einsum('bhts,bshd->bthd', attn, v).reshape(b, t, OUT_SIZE)
        cat_tgt = jnp.concatenate([tgt, tgt_update], axis=2)
        return jnp.einsum('btf,of->bto', cat_tgt, W_out) + b_out

    def _L0_ffn_ref(x, Wqkv, q_scale, k_scale, Wo, ln_g, ln_b, W1, b1, W2, b2):
        import jax, jax.numpy as jnp
        import numpy as np
        DIM = 128
        DEPTH = 6
        HEADS = 16
        DIM_HEAD = 64
        WINDOW = 32
        INNER = HEADS * DIM_HEAD
        DIM_INNER = int(DIM * 4 * 2 / 3)
        QK_SCALE = 8.0

        def shift_tokens(t):
            a, s = jnp.split(t, 2, -1)
            s = jnp.pad(s, ((0, 0), (1, 0), (0, 0)))[:, :-1]
            return jnp.concatenate([a, s], -1)

        def l2norm(t):
            return t / jnp.maximum(jnp.linalg.norm(t, axis=-1, keepdims=True), 1e-12)

        def rotate_half(x):
            x1, x2 = jnp.split(x, 2, -1)
            return jnp.concatenate([-x2, x1], -1)

        def rotary_tables(n):
            half = jnp.arange(0, DIM_HEAD, 2, dtype=jnp.float32)
            inv_freq = 1.0 / 10000.0 ** (half / DIM_HEAD)
            t = jnp.arange(n, dtype=jnp.float32)
            freqs = t[:, None] * inv_freq[None, :]
            freqs = jnp.concatenate([freqs, freqs], -1)
            base_scale = (half + 0.4 * DIM_HEAD) / (1.4 * DIM_HEAD)
            power = (t - n // 2) / (WINDOW // 2)
            scale = base_scale[None, :] ** power[:, None]
            scale = jnp.concatenate([scale, scale], -1)
            return (freqs, scale)

        def local_attention(q, k, v):
            b, h, n, d = q.shape
            w = WINDOW
            nw = n // w
            bq = q.reshape(b, h, nw, w, d)
            bk = k.reshape(b, h, nw, w, d)
            bv = v.reshape(b, h, nw, w, d)

            def look(t):
                p = jnp.pad(t, ((0, 0), (0, 0), (1, 0), (0, 0), (0, 0)))
                return jnp.concatenate([p[:, :, :nw], p[:, :, 1:]], axis=3)
            bk2, bv2 = (look(bk), look(bv))
            seq = jnp.arange(n).reshape(nw, w)
            seq_p = jnp.pad(seq, ((1, 0), (0, 0)), constant_values=-1)
            jt = jnp.concatenate([seq_p[:nw], seq_p[1:]], axis=1)
            it = seq[:, :, None]
            jb = jt[:, None, :]
            mask = (it < jb) | (it > jb + w) | (jb == -1)
            sim = jnp.einsum('bhwie,bhwje->bhwij', bq, bk2) * QK_SCALE
            sim = jnp.where(mask, -jnp.finfo(sim.dtype).max, sim)
            attn = jax.nn.softmax(sim, -1)
            out = jnp.einsum('bhwij,bhwje->bhwie', attn, bv2)
            return out.reshape(b, h, n, d)

        def attn_layer(x, Wqkv, qs, ksc, Wo):
            b, n, _ = x.shape
            qkv = x @ Wqkv
            q, k, v = jnp.split(qkv, 3, -1)
            sh = lambda t: t.reshape(b, n, HEADS, DIM_HEAD).transpose(0, 2, 1, 3)
            q, k, v = (sh(q), sh(k), sh(v))
            q = l2norm(q) * qs
            k = l2norm(k) * ksc
            freqs, scale = rotary_tables(n)
            cos, sin = (jnp.cos(freqs), jnp.sin(freqs))
            q = q * cos * scale + rotate_half(q) * sin * scale
            inv = 1.0 / scale
            k = k * cos * inv + rotate_half(k) * sin * inv
            out = local_attention(q, k, v)
            out = out.transpose(0, 2, 1, 3).reshape(b, n, INNER)
            return out @ Wo

        def ffn_layer(x, g, bln, W1, b1, W2, b2):
            mu = x.mean(-1, keepdims=True)
            var = ((x - mu) ** 2).mean(-1, keepdims=True)
            xn = (x - mu) / jnp.sqrt(var + 1e-05) * g + bln
            hg = xn @ W1 + b1
            a, gate = jnp.split(hg, 2, -1)
            return a * jax.nn.gelu(gate, approximate=False) @ W2 + b2
        for i in range(DEPTH):
            x = attn_layer(shift_tokens(x), Wqkv[i], q_scale[i], k_scale[i], Wo[i]) + x
            x = ffn_layer(shift_tokens(x), ln_g[i], ln_b[i], W1[i], b1[i], W2[i], b2[i]) + x
        return x
    x = x + _L0_attn_ref(_layernorm(x, axis=-1), L0_attn_Wa_w, L0_attn_Wa_b, L0_attn_log_gamma, L0_attn_WB_w, L0_attn_WB_b, L0_attn_WC_w, L0_attn_WC_b, L0_attn_D_skip, L0_attn_ln_w, L0_attn_ln_b)
    x = x + _L0_xattn_ref(ctx_2048, _layernorm(x, axis=-1), mask_BxS2_fk1, mask_BxS2_fk1, L0_xattn_W_src, L0_xattn_b_src, L0_xattn_W_tgt, L0_xattn_b_tgt, L0_xattn_W_out, L0_xattn_b_out)
    x = x + _L0_ffn_ref(_layernorm(x, axis=-1), L0_ffn_Wqkv, L0_ffn_q_scale, L0_ffn_k_scale, L0_ffn_Wo, L0_ffn_ln_g, L0_ffn_ln_b, L0_ffn_W1, L0_ffn_b1, L0_ffn_W2, L0_ffn_b2)
    return x

_drawn_inputs = setup_inputs


def setup_inputs(seed=0):
    import zlib

    import numpy as np

    out = dict(_drawn_inputs(seed))
    spreads = {'L0_attn_Wa_b': (0.0, 2.0),
     'L0_attn_ln_w': (1.0, 0.6),
     'L0_attn_ln_b': (0.0, 0.8),
     'L0_xattn_b_src': (0.0, 0.1),
     'L0_xattn_b_tgt': (0.0, 0.695),
     'L0_xattn_b_out': (0.0, 0.1),
     'L0_ffn_q_scale': (1.0, 0.6),
     'L0_ffn_k_scale': (1.0, 0.6),
     'L0_ffn_ln_g': (1.0, 0.6),
     'L0_ffn_ln_b': (0.0, 0.8),
     'L0_ffn_b1': (0.0, 0.8),
     'L0_ffn_b2': (0.0, 0.1)}
    factors = {'L0_attn_Wa_w': 5.304,
     'L0_attn_WB_b': 8.0,
     'L0_attn_D_skip': 5.621,
     'L0_ffn_W1': 4.146,
     'L0_ffn_W2': 4.064}
    for name, (base, spread) in spreads.items():
        noise = np.random.default_rng([zlib.crc32(name.encode()), seed]).standard_normal(out[name].shape)
        drawn = base * np.exp(spread * noise) if base else spread * noise
        out[name] = jnp.asarray(drawn.astype(out[name].dtype))
    for name, factor in factors.items():
        out[name] = (out[name] * factor).astype(out[name].dtype)
    return out
```

```python
from contextlib import ExitStack

import concourse.bass as bass
from concourse import mybir

F32 = mybir.dt.float32
F32R = mybir.dt.float32r
BF16 = mybir.dt.bfloat16
I32 = mybir.dt.int32
ALU = mybir.AluOpType
ACT = mybir.ActivationFunctionType
AX = mybir.AxisListType

P = 128
B = 8
T = 256
D = 128
NT = T // P
ST = 32
SLOT = ST // 2
CF = 256
XH = 8
XD = D // XH
S = 256
L = 6
H = 16
DH = 64
INNER = H * DH
G = INNER // P
W = 32
NW = T // W
QW = P // W
CH = 512
QKV = 3 * INNER
NCH = QKV // CH
STAGE = 5
FI = int(D * 4 * 2 / 3)
FK = [(0, 128), (128, 128), (256, FI - 256)]
QK_SCALE = 8.0
EPS = 1e-5
NEG = -1e30
RSQRT_MAGIC = float(0x5F3759DF)
NEWTON = 3
NEWTON_OPS = 2 + 3 * NEWTON
MADE = 17


class Count:

    def __init__(self, sem, per):
        self.sem, self.per = sem, per

    def at(self, unit, n):
        v = unit * self.per + n
        return max(v, 0) if isinstance(v, int) else v


class Chain:

    def __init__(self, sem, per=0, passed=None):
        self.sem, self.per, self.n, self.passed = sem, per, 0, passed

    def begin(self, unit):
        self.unit, self.n = unit, 0

    def link(self, eng, ins):
        ins.then_inc(self.sem, 1)
        self.n += 1
        eng.wait_ge(self.sem, self.unit * self.per + self.n)

    def apart(self, eng):
        eng.sem_inc(self.passed, 1)


def rsqrt(nc, dve, chain, y, x, t, y_int, x_int, floor, add):
    chain.link(dve, nc.vector.tensor_scalar(x, x, floor, add, ALU.max, ALU.add))
    chain.link(dve, nc.vector.tensor_scalar(y_int, x_int, -0.5, RSQRT_MAGIC, ALU.mult, ALU.add))
    for _ in range(NEWTON):
        chain.link(dve, nc.vector.tensor_tensor(t, y, y, ALU.mult))
        chain.link(dve, nc.vector.scalar_tensor_tensor(t, t, -0.5, x, ALU.mult, ALU.mult))
        chain.link(dve, nc.vector.scalar_tensor_tensor(y, t, 1.5, y, ALU.add, ALU.mult))


def layer_stage(nc, sb, bank, ident, identb, passed, sem, ap, XT):
    wst = sb("w_stage", [P, STAGE, CH])
    wh = sb("w_hi", [P, NCH, CH], F32R)
    wl = sb("w_lo", [P, NCH, CH], F32R)
    wo = sb("w_o", [P, G, D])
    w1 = sb("w_1", [P, 2 * FI])
    w2 = sb("w_2", [P, len(FK), D])
    par_ln = sb("ln_params", [P, 2])
    par_b1 = sb("b1_cols", [P, 2, len(FK)])
    par_b2 = sb("b2_col", [P, 1])
    scales = sb("qk_scales", [P, 2, 2, DH])
    base = sb("rotary_base", [P, 2, 2, NT, DH])
    tab = sb("rotary_tables", [P, 2, 2, NT, DH])
    xh = sb("xs_hi", [P, T], F32R)
    xl = sb("xs_lo", [P, T], F32R)
    sq = sb("squares", [P, 2, CH])
    tc = sb("times_cos", [P, 2, CH])
    ts = sb("times_sin", [P, 2, CH])
    U = sb("rotated", [P, NT, 4, CH])
    ss = sb("sum_squares", [P, NT, 2 * H])
    rn = sb("inv_norm", [P, NT, 2 * H])
    nt_ = sb("newton_tmp", [P, NT, 2 * H])
    qT = [sb(f"qT{p}", [P, G, T]) for p in range(2)]
    kT = [sb(f"kT{p}", [P, G, W + T]) for p in range(2)]
    vn = sb("v_tokens", [P, NT, 2, CH])
    vw = [sb(f"v_windows{p}", [P, NW, CH]) for p in range(2)]
    prob = [sb(f"prob{t}", [P, G, 2, DH]) for t in range(NT)]
    mx = sb("row_max", [P, NT, 2, G])
    sm = sb("row_sum", [P, NT, G, 2])
    rs = sb("inv_sum", [P, NT, G, 2])
    pT = [sb(f"probT{t}", [P, G, P]) for t in range(NT)]
    oT = [sb(f"oT{p}", [P, G, T]) for p in range(2)]
    xs = sb("x_shifted", [P, 1 + T])
    st = sb("ln_stats", [P, NT, 6])
    mv = sb("ln_mean_var", [P, NT, 2])
    rv = sb("ln_rstd", [P, NT, 2])
    rt = sb("ln_tmp", [P, NT, 2])
    xn = sb("x_norm", [P, NT, D])
    xnT = sb("x_normT", [P, T])
    act_ = sb("ffn_hidden", [P, len(FK), T])
    maskb = sb("window_mask", [P, NT, DH], BF16)

    Dk, C, A, Bk, E = bank[0:2], bank[2], bank[3:5], bank[5:7], bank[7]

    def cnt(name, per):
        return Count(sem(name), per)

    const = sem("consts_loaded")
    made = sem("consts_made")
    wdma = [cnt(f"wqkv_chunk_loaded{c}", 16) for c in range(NCH)]
    whi = cnt("wqkv_hi", NCH)
    wlo = cnt("wqkv_lo", NCH)
    fdma = cnt("ffn_weights_loaded", 16 * 11)
    sdma = cnt("qk_scales_loaded", 16 * 6)
    tabs = cnt("rotary_tables_made", 4)
    xs_hi = cnt("xs_hi_made", 2)
    xs_lo = cnt("xs_lo_made", 2)
    proj = cnt("proj_done", 12)
    squared = cnt("squared", 8)
    summed = cnt("squares_summed", 8)
    rot = cnt("rotary_products", 8)
    added = cnt("rotary_added", 8)
    normed = cnt("inv_norm_made", 2)
    scaled = cnt("qk_normalised", 8)
    turned = cnt("qk_transposed", 8)
    kept = cnt("qkT_kept", 8)
    v_kept = cnt("v_kept", 4)
    v_spread = [cnt("v_spread_tile0", 16 * 16), cnt("v_spread_tile1", 16 * 14)]
    c1 = Chain(sem("chain_norms"), 2 * NEWTON_OPS)
    scored = cnt("scores_done", 4)
    maxed = cnt("max_done", 4)
    shifted = cnt("max_taken_off", 4)
    exped = cnt("exp_done", 2)
    sumd = cnt("row_sums", 2)
    inved = cnt("inv_sums", 2)
    p_turned = cnt("probs_transposed", 4)
    p_kept = cnt("probT_kept", 4)
    pv = cnt("pv_done", 4)
    o_kept = cnt("out_normalised", 4)
    o_turned = cnt("out_transposed", 4)
    oT_kept = cnt("outT_kept", 4)
    wo_done = cnt("wo_done", 1)
    x1_made = cnt("x1_made", 2)
    lna = cnt("ln_tokens_done", 1)
    c3 = Chain(sem("chain_ln"), 2 + NEWTON_OPS, passed)
    xn_made = cnt("xn_made", 2)
    lnb = cnt("xnT_done", 1)
    xnT_kept = cnt("xnT_kept", 1)
    hid = cnt("hidden_done", 3)
    gated = cnt("gelu_done", 3)
    hact = cnt("hidden_gated", 3)
    w2_done = cnt("w2_done", 1)
    fin = cnt("layer_out", 2)

    wq_d, wo_d, w1_d, w2_d = ap["Wqkv"], ap["Wo"], ap["W1"], ap["W2"]
    qs_d = [ap["q_scale"], ap["k_scale"]]
    U1, L1 = slice(0, 64), slice(64, 128)

    def pairs_view(t):
        return t.rearrange("p (h a d) -> p h a d", a=2, d=DH // 2)

    ALL = (True, True, True)

    def units(eng, body, layer_start, ffn_switch):
        layer_start(0)
        body(0, 0, 0, (True, False, False), True)
        body(1, 1, 1, (True, True, False), True)
        ffn_switch(0)
        body(2, 2, 0, ALL, True)
        body(3, 3, 1, ALL, True)
        with eng.Fori(2, B // 2) as m:
            for p in range(2):
                body(m * 2 + p, m * 2 + p, p, ALL, True)
        with eng.Fori(1, L) as l:
            layer_start(l)
            for p in range(2):
                body(l * B + p, p, p, ALL, False)
            ffn_switch(l)
            with eng.Fori(1, B // 2) as m:
                for p in range(2):
                    body(l * B + m * 2 + p, m * 2 + p, p, ALL, False)
        n = L * B
        body(n, 0, 0, (False, True, True), False)
        body(n + 1, 1, 1, (False, False, True), False)

    def nothing(l):
        pass

    with nc.Block() as block:

        @block.sync
        def _(sp):
            sp.dma_start(base[:, :, :, :, :], ap["rotary"].rearrange("q s (t p) d -> p q s t d", p=P)).then_inc(const, 16)

            def load_qkv_chunk(l, c):
                dst = wst[:, c % STAGE, :]
                if c < 4:
                    src = wq_d[l, :, c * CH:(c + 1) * CH]
                else:
                    src = wq_d[l, :, 2 * INNER:].rearrange("k (g a d) -> k a g d", a=2, d=DH)[:, c - 4, :, :]
                    dst = dst.rearrange("k (g d) -> k g d", d=DH)
                sp.dma_start(dst, src).then_inc(wdma[c].sem, 16)

            def load_ffn(l):
                sp.wait_ge(w2_done.sem, w2_done.at(l * B, 0))
                sp.sem_inc(passed, 1)
                sp.wait_ge(fin.sem, fin.at(l * B, 0))
                s = fdma.sem
                sp.dma_start(wo[:, :, :], wo_d[l].rearrange("(g p) n -> p g n", p=P)).then_inc(s, 16)
                sp.dma_start(w1[:, :], w1_d[l]).then_inc(s, 16)
                sp.dma_start(w2[:, 0:2, :], w2_d[l, 0:256, :].rearrange("(k p) n -> p k n", p=P)).then_inc(s, 16)
                sp.dma_start(w2[0:FK[2][1], 2, :], w2_d[l, 256:FI, :]).then_inc(s, 16)
                sp.dma_start(par_ln[:, 0:1], ap["ln_g"][l].rearrange("(p a) -> p a", a=1),
                             allow_slow_non_contiguous=True).then_inc(s, 16)
                sp.dma_start(par_ln[:, 1:2], ap["ln_b"][l].rearrange("(p a) -> p a", a=1),
                             allow_slow_non_contiguous=True).then_inc(s, 16)
                for a in range(2):
                    sp.dma_start(par_b1[:, a, 0:2], ap["b1"][l, a * FI:a * FI + 256].rearrange("(k p) -> p k", p=P),
                                 allow_slow_non_contiguous=True).then_inc(s, 16)
                    sp.dma_start(par_b1[0:FK[2][1], a, 2:3],
                                 ap["b1"][l, a * FI + 256:(a + 1) * FI].rearrange("(p a) -> p a", a=1),
                             allow_slow_non_contiguous=True).then_inc(s, 16)
                sp.dma_start(par_b2[:, :], ap["b2"][l].rearrange("(p a) -> p a", a=1),
                             allow_slow_non_contiguous=True).then_inc(s, 16)

            def load_first_chunks(l):
                sp.wait_ge(wlo.sem, wlo.at(l, 0))
                for c in range(STAGE):
                    load_qkv_chunk(l, c)

            def load_last_chunks(l):
                for c in range(STAGE, NCH):
                    sp.wait_ge(wlo.sem, wlo.at(l, c - STAGE + 1))
                    load_qkv_chunk(l, c)

            def load_scales(l):
                sp.wait_ge(tabs.sem, tabs.at(l, 0))
                for q in range(2):
                    row = qs_d[q][l].rearrange("(a n) -> a n", a=1)
                    sp.dma_start(scales[:, q, 0, :], row.broadcast_to([P, DH])).then_inc(sdma.sem, 16)
                    for a in range(2):
                        half = row[:, (1 - a) * 32:(2 - a) * 32]
                        sp.dma_start(scales[:, q, 1, a * 32:a * 32 + 32], half.broadcast_to([P, DH // 2])).then_inc(sdma.sem, 16)

            def spread_v(u, p, t):
                sp.wait_ge(v_kept.sem, v_kept.at(u, 2 * t + 2))
                sp.wait_ge(pv.sem, pv.at(u - 1, 0))
                for c in range(QW * t, QW * (t + 1)):
                    src = vn[W * (c % QW):W * (c % QW) + W, t, :, :]
                    for kb, w in ((1, c), (0, c + 1)):
                        if w == NW:
                            continue
                        for a in range(2):
                            row = 64 * a + W * kb
                            sp.dma_start(vw[p][row:row + W, w, :], src[:, a, :]).then_inc(v_spread[t].sem, 16)

            def body(i, j, p, on, layer0):
                if on[0]:
                    for t in range(NT):
                        spread_v(i, p, t)

            def layer(l):
                load_last_chunks(l)
                load_scales(l)
                for p in range(2):
                    body(l * B + p, p, p, ALL, False)
                load_ffn(l)
                load_first_chunks(l + 1)
                with sp.Fori(1, B // 2) as m:
                    for p in range(2):
                        body(l * B + m * 2 + p, m * 2 + p, p, ALL, False)

            load_first_chunks(0)
            load_scales(0)
            load_last_chunks(0)
            for p in range(2):
                body(p, p, p, ALL, True)
            load_ffn(0)
            load_first_chunks(1)
            for p in range(2):
                body(2 + p, 2 + p, p, ALL, True)
            with sp.Fori(2, B // 2) as m:
                for p in range(2):
                    body(m * 2 + p, m * 2 + p, p, ALL, True)
            with sp.Fori(1, L - 1) as l:
                layer(l)
            last = L - 1
            load_last_chunks(last)
            load_scales(last)
            for p in range(2):
                body(last * B + p, p, p, ALL, False)
            load_ffn(last)
            with sp.Fori(1, B // 2) as m:
                for p in range(2):
                    body(last * B + m * 2 + p, m * 2 + p, p, ALL, False)

        @block.gpsimd
        def _(pool):
            c = Chain(made)
            c.begin(0)

            def do(ins):
                c.link(pool, ins)

            do(nc.gpsimd.memset(xs[:, :], 0.0))
            for p in range(2):
                do(nc.gpsimd.memset(kT[p][:, :, 0:W], 0.0))
                for a in range(2):
                    do(nc.gpsimd.memset(vw[p][64 * a:64 * a + W, 0, :], 0.0))
            do(nc.gpsimd.memset(maskb[:, :, :], 0.0))
            for w in range(QW):
                rows = maskb[W * w:W * w + W, :, :]
                do(nc.gpsimd.affine_select(out=rows, in_=rows, compare_op=ALU.is_ge, fill=NEG, base=0,
                                           pattern=[[0, NT], [1, 2 * W]], channel_multiplier=-1))
                do(nc.gpsimd.affine_select(out=rows, in_=rows, compare_op=ALU.is_ge, fill=NEG, base=W,
                                           pattern=[[0, NT], [-1, 2 * W]], channel_multiplier=1))
            do(nc.gpsimd.memset(maskb[0:W, 0, 0:W], NEG))
            assert c.n == MADE
            pool.wait_ge(const, 16)

            def tables(l):
                pool.wait_ge(sdma.sem, sdma.at(l, 16 * 6))
                pool.wait_ge(rot.sem, rot.at(l * B, 0))
                for q in range(2):
                    for s in range(2):
                        sc = scales[:, q, s, :].unsqueeze(1).broadcast_to([P, NT, DH])
                        nc.gpsimd.tensor_tensor(tab[:, q, s, :, :], base[:, q, s, :, :], sc, ALU.mult).then_inc(tabs.sem, 1)

            def add(u, f):
                pool.wait_ge(rot.sem, rot.at(u, f + 1))
                pool.wait_ge(turned.sem, turned.at(u - 1, f + 1))
                nc.gpsimd.tensor_tensor(U[:, f // 4, f % 4, :], tc[:, f % 2, :], ts[:, f % 2, :], ALU.add).then_inc(added.sem, 1)

            def norm(u, f):
                t, c = f // 4, f % 4
                pool.wait_ge(normed.sem, normed.at(u, t + 1))
                pool.wait_ge(added.sem, added.at(u, f + 1))
                v = U[:, t, c, :].rearrange("p (h d) -> p h d", d=DH)
                r = rn[:, t, 8 * c:8 * c + 8].unsqueeze(2).broadcast_to([P, 8, DH])
                nc.gpsimd.tensor_tensor(v, v, r, ALU.mult).then_inc(scaled.sem, 1)

            def body(i, j, p, on, layer0):
                if on[0]:
                    for t in range(NT):
                        for f in range(4):
                            add(i, 4 * t + f)
                        for f in range(4):
                            norm(i, 4 * t + f)
            units(pool, body, tables, nothing)

        @block.scalar
        def _(act):
            act.wait_ge(made, MADE)

            def split_weights(l):
                act.wait_ge(proj.sem, proj.at(l * B, 0))
                for c in range(NCH):
                    act.wait_ge(wdma[c].sem, wdma[c].at(l, 16))
                    nc.scalar.activation(wh[:, c, :], wst[:, c % STAGE, :], ACT.Copy).then_inc(whi.sem, 1)

            def x_hi(u, j, layer0):
                if not layer0:
                    act.wait_ge(fin.sem, fin.at(u - B, 2))
                act.wait_ge(proj.sem, proj.at(u, 0))
                nc.scalar.activation(xh[U1, :], XT[U1, j, 1:1 + T], ACT.Copy).then_inc(xs_hi.sem, 1)
                nc.scalar.activation(xh[L1, :], XT[L1, j, 0:T], ACT.Copy).then_inc(xs_hi.sem, 1)

            def square(u, k):
                f = k // 6 * 4 + k % 6
                act.wait_ge(proj.sem, proj.at(u, k + 1))
                act.wait_ge(summed.sem, summed.at(u, f - 1))
                nc.scalar.activation(sq[:, f % 2, :], Dk[k % 2][:, :], ACT.Square).then_inc(squared.sem, 1)

            def keep_v(u, k):
                t, a = k // 6, k % 6 - 4
                act.wait_ge(proj.sem, proj.at(u, k + 1))
                act.wait_ge(v_spread[t].sem, v_spread[t].at(u, 0))
                nc.scalar.activation(vn[:, t, a, :], Dk[k % 2][:, :], ACT.Copy).then_inc(v_kept.sem, 1)

            def keep_qk(u, p, f):
                t, c = f // 4, f % 4
                act.wait_ge(turned.sem, turned.at(u, f + 1))
                act.wait_ge(scored.sem, scored.at(u - 1, 0))
                src = C[:, :].rearrange("p (g n) -> p g n", n=P)
                g = 4 * (c % 2)
                if c < 2:
                    dst = qT[p][:, g:g + 4, t * P:(t + 1) * P]
                else:
                    dst = kT[p][:, g:g + 4, W + t * P:W + (t + 1) * P]
                nc.scalar.activation(dst, src, ACT.Copy).then_inc(kept.sem, 1)

            def exp(u, t):
                act.wait_ge(shifted.sem, shifted.at(u, 2 * t + 2))
                nc.scalar.activation(prob[t][:, :, :, :], prob[t][:, :, :, :], ACT.Exp, scale=QK_SCALE).then_inc(exped.sem, 1)

            def keep_pT(u, t, h):
                act.wait_ge(p_turned.sem, p_turned.at(u, 2 * t + h + 1))
                act.wait_ge(pv.sem, pv.at(u - 1, 2 * t + 2))
                nc.scalar.activation(pT[t][:, 4 * h:4 * h + 4, :], Bk[h][:, :].rearrange("p (g n) -> p g n", n=P),
                                     ACT.Copy).then_inc(p_kept.sem, 1)

            def keep_oT(u, p, t, h):
                act.wait_ge(o_turned.sem, o_turned.at(u, 2 * t + h + 1))
                act.wait_ge(wo_done.sem, wo_done.at(u - 1, 0))
                nc.scalar.activation(oT[p][:, 4 * h:4 * h + 4, t * P:(t + 1) * P],
                                     Bk[h][:, :].rearrange("p (g n) -> p g n", n=P), ACT.Copy).then_inc(oT_kept.sem, 1)

            def keep_xnT(u):
                act.wait_ge(lnb.sem, lnb.at(u, 1))
                nc.scalar.activation(xnT[:, :], E[:, 0:T], ACT.Identity, scale=par_ln[:, 0:1],
                                     bias=par_ln[:, 1:2]).then_inc(xnT_kept.sem, 1)

            def gelu(u, k):
                m = FK[k][1]
                act.wait_ge(hid.sem, hid.at(u, k + 1))
                nc.scalar.activation(act_[0:m, k, :], E[0:m, T:2 * T], ACT.Gelu, bias=par_b1[0:m, 1, k:k + 1]).then_inc(gated.sem, 1)

            def body(i, j, p, on, layer0):
                s1, s2, s3 = on
                a, b, q = i - 1, i - 2, 1 - p
                if s1:
                    x_hi(i, j, layer0)
                    square(i, 0)
                    square(i, 1)
                if s1:
                    square(i, 2)
                    square(i, 3)
                if s2:
                    exp(a, 0)
                    keep_pT(a, 0, 0)
                    keep_pT(a, 0, 1)
                if s1:
                    keep_v(i, 4)
                    keep_v(i, 5)
                if s3:
                    keep_xnT(b)
                if s1:
                    square(i, 6)
                    square(i, 7)
                if s2:
                    keep_oT(a, q, 0, 0)
                    keep_oT(a, q, 0, 1)
                if s3:
                    gelu(b, 0)
                if s1:
                    keep_qk(i, p, 0)
                    keep_qk(i, p, 1)
                    square(i, 8)
                    square(i, 9)
                    keep_qk(i, p, 2)
                    keep_qk(i, p, 3)
                if s2:
                    exp(a, 1)
                    keep_pT(a, 1, 0)
                    keep_pT(a, 1, 1)
                if s3:
                    gelu(b, 1)
                if s1:
                    keep_v(i, 10)
                    keep_v(i, 11)
                if s3:
                    gelu(b, 2)
                if s1:
                    keep_qk(i, p, 4)
                    keep_qk(i, p, 5)
                if s2:
                    keep_oT(a, q, 1, 0)
                    keep_oT(a, q, 1, 1)
                if s1:
                    keep_qk(i, p, 6)
                    keep_qk(i, p, 7)
            units(act, body, split_weights, nothing)

        @block.tensor
        def _(pe):
            pe.wait_ge(made, MADE)

            def project(u, k):
                t, c = k // 6, k % 6
                if k == 0:
                    pe.wait_ge(xs_lo.sem, xs_lo.at(u, 2))
                kk, uu = (k - 2, u) if k >= 2 else (k + 10, u - 1)
                tt, cc = kk // 6, kk % 6
                if cc < 4:
                    pe.wait_ge(rot.sem, rot.at(uu, 4 * tt + cc + 1))
                else:
                    pe.wait_ge(v_kept.sem, v_kept.at(uu, 2 * tt + cc - 4 + 1))
                out = Dk[k % 2][:, :]
                tok = slice(t * P, (t + 1) * P)
                nc.tensor.matmul(out, xh[:, tok], wh[:, c, :], start=True, stop=False)
                nc.tensor.matmul(out, xh[:, tok], wl[:, c, :], start=False, stop=False)
                nc.tensor.matmul(out, xl[:, tok], wh[:, c, :], start=False, stop=True).then_inc(proj.sem, 1)

            def turn_qk(u, f):
                t, c = f // 4, f % 4
                pe.wait_ge(scaled.sem, scaled.at(u, f + 1))
                pe.wait_ge(kept.sem, kept.at(u, f))
                for g in range(4):
                    mm = nc.tensor.transpose(C[:, g * P:(g + 1) * P], U[:, t, c, g * P:(g + 1) * P], ident[:, :])
                mm.then_inc(turned.sem, 1)

            def scores(u, p, t):
                pe.wait_ge(kept.sem, kept.at(u, 4 * (t + 1)))
                pe.wait_ge(o_kept.sem, o_kept.at(u, 2 * t))
                for a in range(2):
                    nc.tensor.matmul(A[a][:, :], identb[:, :], maskb[:, t, :].unsqueeze(1).broadcast_to([P, G, DH]),
                                     start=True, stop=False, skip_group_check=True)
                for g in range(G):
                    for w in range(QW):
                        for a in range(2):
                            row = 64 * a
                            col = t * P + W * w
                            mm = nc.tensor.matmul(A[a][W * w:W * w + W, g * DH:(g + 1) * DH],
                                                  qT[p][row:row + 64, g, col:col + W],
                                                  kT[p][row:row + 64, g, col:col + 2 * W],
                                                  start=False, stop=True, skip_group_check=True)
                            if g == G - 1 and w == QW - 1:
                                mm.then_inc(scored.sem, 1)

            def turn_p(u, t, h):
                pe.wait_ge(exped.sem, exped.at(u, t + 1))
                if t == 0:
                    pe.wait_ge(oT_kept.sem, oT_kept.at(u - 1, 2 + h + 1))
                else:
                    pe.wait_ge(oT_kept.sem, oT_kept.at(u, h + 1))
                for g in range(4):
                    mm = nc.tensor.transpose(Bk[h][:, g * P:(g + 1) * P],
                                             prob[t][:, 4 * h + g, :, :].rearrange("p a d -> p (a d)"), ident[:, :])
                mm.then_inc(p_turned.sem, 1)

            def values(u, p, t):
                pe.wait_ge(p_kept.sem, p_kept.at(u, 2 * t + 2))
                pe.wait_ge(v_spread[0].sem, v_spread[0].at(u, 16 * 16))
                if t:
                    pe.wait_ge(v_spread[1].sem, v_spread[1].at(u, 16 * 14))
                pe.sem_inc(passed, 1)
                for g in range(G):
                    for w in range(QW):
                        for a in range(2):
                            row = 64 * a
                            mm = nc.tensor.matmul(A[a][W * w:W * w + W, g * DH:(g + 1) * DH],
                                                  pT[t][row:row + 64, g, W * w:W * w + W],
                                                  vw[p][row:row + 64, QW * t + w, g * DH:(g + 1) * DH],
                                                  start=True, stop=True, skip_group_check=True)
                            if g == G - 1 and w == QW - 1:
                                mm.then_inc(pv.sem, 1)

            def turn_o(u, t, h):
                pe.wait_ge(o_kept.sem, o_kept.at(u, 2 * t + 2))
                pe.wait_ge(p_kept.sem, p_kept.at(u, 2 * t + h + 1))
                for g in range(4):
                    mm = nc.tensor.transpose(Bk[h][:, g * P:(g + 1) * P],
                                             prob[t][:, 4 * h + g, :, :].rearrange("p a d -> p (a d)"), ident[:, :])
                mm.then_inc(o_turned.sem, 1)

            def out_proj(u, p):
                pe.wait_ge(oT_kept.sem, oT_kept.at(u, 4))
                pe.wait_ge(fin.sem, fin.at(u, 0))
                for g in range(G):
                    mm = nc.tensor.matmul(E[:, 0:T], wo[:, g, :], oT[p][:, g, :], start=(g == 0), stop=(g == G - 1))
                mm.then_inc(wo_done.sem, 1)

            def ln_tokens(u):
                pe.wait_ge(x1_made.sem, x1_made.at(u, 2))
                for t in range(NT):
                    mm = nc.tensor.transpose(E[:, t * P:(t + 1) * P], xs[:, t * P:(t + 1) * P], ident[:, :])
                mm.then_inc(lna.sem, 1)

            def ln_back(u):
                pe.wait_ge(xn_made.sem, xn_made.at(u, 2))
                for t in range(NT):
                    mm = nc.tensor.transpose(E[:, t * P:(t + 1) * P], xn[:, t, :], ident[:, :])
                mm.then_inc(lnb.sem, 1)

            def hidden(u, k):
                o, m = FK[k]
                if k == 0:
                    pe.wait_ge(xnT_kept.sem, xnT_kept.at(u, 1))
                else:
                    pe.wait_ge(hact.sem, hact.at(u, k))
                nc.tensor.matmul(E[0:m, 0:T], w1[:, o:o + m], xnT[:, :], start=True, stop=True)
                nc.tensor.matmul(E[0:m, T:2 * T], w1[:, FI + o:FI + o + m], xnT[:, :], start=True, stop=True).then_inc(hid.sem, 1)

            def ffn_out(u):
                pe.wait_ge(hact.sem, hact.at(u, 3))
                for k, (o, m) in enumerate(FK):
                    mm = nc.tensor.matmul(E[:, 0:T], w2[0:m, k, :], act_[0:m, k, :], start=(k == 0), stop=(k == 2))
                mm.then_inc(w2_done.sem, 1)

            def body(i, j, p, on, layer0):
                s1, s2, s3 = on
                a, b, q = i - 1, i - 2, 1 - p
                if s2:
                    scores(a, q, 0)
                if s1:
                    project(i, 0)
                    project(i, 1)
                if s3:
                    out_proj(b, p)
                if s1:
                    project(i, 2)
                    project(i, 3)
                if s2:
                    turn_p(a, 0, 0)
                    turn_p(a, 0, 1)
                if s3:
                    ln_tokens(b)
                if s1:
                    project(i, 4)
                    project(i, 5)
                if s2:
                    values(a, q, 0)
                if s3:
                    ln_back(b)
                if s1:
                    project(i, 6)
                    project(i, 7)
                if s2:
                    turn_o(a, 0, 0)
                    turn_o(a, 0, 1)
                if s3:
                    hidden(b, 0)
                if s2:
                    scores(a, q, 1)
                if s1:
                    turn_qk(i, 0)
                    turn_qk(i, 1)
                    project(i, 8)
                    project(i, 9)
                    turn_qk(i, 2)
                    turn_qk(i, 3)
                if s2:
                    turn_p(a, 1, 0)
                    turn_p(a, 1, 1)
                if s3:
                    hidden(b, 1)
                if s1:
                    project(i, 10)
                    project(i, 11)
                if s2:
                    values(a, q, 1)
                if s3:
                    hidden(b, 2)
                if s1:
                    turn_qk(i, 4)
                    turn_qk(i, 5)
                if s2:
                    turn_o(a, 1, 0)
                    turn_o(a, 1, 1)
                if s3:
                    ffn_out(b)
                if s1:
                    turn_qk(i, 6)
                    turn_qk(i, 7)

            def weights(l):
                pe.wait_ge(wlo.sem, wlo.at(l, NCH))

            def ffn_weights(l):
                pe.wait_ge(fdma.sem, fdma.at(l, 16 * 11))
                pe.sem_inc(passed, 1)
            units(pe, body, weights, ffn_weights)

        @block.vector
        def _(dve):
            dve.wait_ge(made, MADE)

            def split_weights(l):
                for c in range(NCH):
                    dve.wait_ge(whi.sem, whi.at(l, c + 1))
                    nc.vector.tensor_tensor(wl[:, c, :], wst[:, c % STAGE, :], wh[:, c, :].bitcast(F32),
                                            ALU.subtract).then_inc(wlo.sem, 1)
                dve.wait_ge(tabs.sem, tabs.at(l, 4))

            def x_lo(u, j):
                dve.wait_ge(xs_hi.sem, xs_hi.at(u, 2))
                nc.vector.tensor_tensor(xl[U1, :], XT[U1, j, 1:1 + T], xh[U1, :].bitcast(F32), ALU.subtract).then_inc(xs_lo.sem, 1)
                nc.vector.tensor_tensor(xl[L1, :], XT[L1, j, 0:T], xh[L1, :].bitcast(F32), ALU.subtract).then_inc(xs_lo.sem, 1)

            def rotate(u, k):
                t, c = k // 6, k % 6
                f = 4 * t + c
                q = c // 2
                dve.wait_ge(squared.sem, squared.at(u, f + 1))
                dve.wait_ge(added.sem, added.at(u, f - 1))
                cos = tab[:, q, 0, t, :].unsqueeze(1).broadcast_to([P, 8, DH])
                sin = tab[:, q, 1, t, :].rearrange("p (a d) -> p a d", a=2).unsqueeze(1).broadcast_to([P, 8, 2, DH // 2])
                nc.vector.tensor_tensor(tc[:, f % 2, :].rearrange("p (h d) -> p h d", d=DH),
                                        Dk[k % 2][:, :].rearrange("p (h d) -> p h d", d=DH), cos, ALU.mult)
                swapped = pairs_view(Dk[k % 2][:, :])[:, :, ::-1, :]
                nc.vector.tensor_tensor(pairs_view(ts[:, f % 2, :]), swapped, sin, ALU.mult).then_inc(rot.sem, 1)
                nc.vector.tensor_reduce(ss[:, t, 8 * c:8 * c + 8], sq[:, f % 2, :].rearrange("p (h d) -> p h d", d=DH),
                                        AX.X, ALU.add).then_inc(summed.sem, 1)

            def inv_norms(u, t):
                dve.wait_ge(summed.sem, summed.at(u, 4 * t + 4))
                dve.wait_ge(scaled.sem, scaled.at(u - 1, 4 * t + 4))
                c1.begin(u)
                c1.n = t * NEWTON_OPS
                y, x, tmp = rn[:, t, :], ss[:, t, :], nt_[:, t, :]
                rsqrt(nc, dve, c1, y, x, tmp, y.bitcast(I32), x.bitcast(I32), 1e-24, 0.0)
                nc.vector.tensor_copy(nt_[:, t, 0:1], rn[:, t, 0:1]).then_inc(normed.sem, 1)

            def row_max(u, t, a):
                dve.wait_ge(scored.sem, scored.at(u, 2 * t + a + 1))
                src = A[a][:, :].rearrange("p (g d) -> p g d", d=DH)
                nc.vector.tensor_reduce(mx[:, t, a, :], src, AX.X, ALU.max).then_inc(maxed.sem, 1)

            def take_max(u, t, a):
                dve.wait_ge(maxed.sem, maxed.at(u, 2 * t + a + 1))
                if a == 0:
                    dve.wait_ge(o_turned.sem, o_turned.at(u - 1, 2 * t + 2))
                src = A[a][:, :].rearrange("p (g d) -> p g d", d=DH)
                nc.vector.tensor_tensor(prob[t][:, :, a, :], src, mx[:, t, a, :].unsqueeze(2).broadcast_to([P, G, DH]),
                                        ALU.subtract).then_inc(shifted.sem, 1)

            def row_sum(u, t):
                dve.wait_ge(exped.sem, exped.at(u, t + 1))
                nc.vector.tensor_reduce(sm[:, t, :, :], prob[t][:, :, :, :], AX.X, ALU.add).then_inc(sumd.sem, 1)
                dve.wait_ge(sumd.sem, sumd.at(u, t + 1))
                nc.vector.reciprocal(rs[:, t, :, :], sm[:, t, :, :]).then_inc(inved.sem, 1)

            def normalise(u, t, a):
                dve.wait_ge(pv.sem, pv.at(u, 2 * t + a + 1))
                dve.wait_ge(inved.sem, inved.at(u, t + 1))
                if a == 0:
                    dve.wait_ge(p_turned.sem, p_turned.at(u, 2 * t + 2))
                src = A[a][:, :].rearrange("p (g d) -> p g d", d=DH)
                nc.vector.tensor_tensor(prob[t][:, :, a, :], src, rs[:, t, :, a].unsqueeze(2).broadcast_to([P, G, DH]),
                                        ALU.mult).then_inc(o_kept.sem, 1)

            def add_attention(u, j):
                dve.wait_ge(wo_done.sem, wo_done.at(u, 1))
                dve.wait_ge(fin.sem, fin.at(u, 0))
                dve.wait_ge(lna.sem, lna.at(u, 0))
                nc.vector.tensor_tensor(xs[U1, 0:T], E[U1, 0:T], XT[U1, j, 1:1 + T], ALU.add).then_inc(x1_made.sem, 1)
                nc.vector.tensor_tensor(xs[L1, 1:1 + T], E[L1, 0:T], XT[L1, j, 1:1 + T], ALU.add).then_inc(x1_made.sem, 1)

            def ln_stats(u):
                dve.wait_ge(lna.sem, lna.at(u, 1))
                dve.wait_ge(lnb.sem, lnb.at(u, 0))
                c3.begin(u)
                for t in range(NT):
                    ins = nc.vector.bn_stats(st[:, t, :], E[:, t * P:(t + 1) * P])
                c3.link(dve, ins)
                c3.apart(dve)
                for t in range(NT):
                    ins = nc.vector.bn_aggr(mv[:, t, :], st[:, t, :])
                c3.link(dve, ins)
                y, x, tmp = rv[:, :, 0], mv[:, :, 1], rt[:, :, 0]
                rsqrt(nc, dve, c3, y, x, tmp, rv[:, :, 0].bitcast(I32), mv[:, :, 1].bitcast(I32), 0.0, EPS)
                for t in range(NT):
                    nc.vector.tensor_scalar(xn[:, t, :], E[:, t * P:(t + 1) * P], mv[:, t, 0:1], rv[:, t, 0:1],
                                            ALU.subtract, ALU.mult).then_inc(xn_made.sem, 1)

            def gate(u, k):
                m = FK[k][1]
                dve.wait_ge(gated.sem, gated.at(u, k + 1))
                dve.wait_ge(w2_done.sem, w2_done.at(u, 0))
                nc.vector.scalar_tensor_tensor(act_[0:m, k, :], E[0:m, 0:T], par_b1[0:m, 0, k:k + 1], act_[0:m, k, :],
                                               ALU.add, ALU.mult).then_inc(hact.sem, 1)

            def layer_out(u, j):
                dve.wait_ge(w2_done.sem, w2_done.at(u, 1))
                dve.wait_ge(x1_made.sem, x1_made.at(u, 2))
                nc.vector.scalar_tensor_tensor(XT[U1, j, 1:1 + T], E[U1, 0:T], par_b2[U1, 0:1], xs[U1, 0:T],
                                               ALU.add, ALU.add).then_inc(fin.sem, 1)
                nc.vector.scalar_tensor_tensor(XT[L1, j, 1:1 + T], E[L1, 0:T], par_b2[L1, 0:1], xs[L1, 1:1 + T],
                                               ALU.add, ALU.add).then_inc(fin.sem, 1)

            def body(i, j, p, on, layer0):
                s1, s2, s3 = on
                a, b, q = i - 1, i - 2, 1 - p
                jb = j + 6 if isinstance(j, int) and j < 2 else j - 2
                if s1:
                    x_lo(i, j)
                if s2:
                    row_max(a, 0, 0)
                    row_max(a, 0, 1)
                    take_max(a, 0, 0)
                    take_max(a, 0, 1)
                if s1:
                    rotate(i, 0)
                    rotate(i, 1)
                if s3:
                    add_attention(b, jb)
                if s1:
                    rotate(i, 2)
                    rotate(i, 3)
                if s2:
                    row_sum(a, 0)
                if s3:
                    ln_stats(b)
                if s1:
                    inv_norms(i, 0)
                if s2:
                    normalise(a, 0, 0)
                    normalise(a, 0, 1)
                if s1:
                    rotate(i, 6)
                    rotate(i, 7)
                if s3:
                    gate(b, 0)
                if s2:
                    row_max(a, 1, 0)
                    row_max(a, 1, 1)
                    take_max(a, 1, 0)
                    take_max(a, 1, 1)
                if s1:
                    rotate(i, 8)
                    rotate(i, 9)
                if s2:
                    row_sum(a, 1)
                if s3:
                    gate(b, 1)
                if s1:
                    inv_norms(i, 1)
                if s2:
                    normalise(a, 1, 0)
                    normalise(a, 1, 1)
                if s3:
                    gate(b, 2)
                    layer_out(b, jb)
            units(dve, body, split_weights, nothing)


def layer_norm_tokens(nc, dve, chain, src, dst, st, mv, rv, rt):
    n = len(src)
    for t in range(n):
        ins = nc.vector.bn_stats(st[:, t, :], src[t])
    chain.link(dve, ins)
    chain.apart(dve)
    for t in range(n):
        ins = nc.vector.bn_aggr(mv[:, t, :], st[:, t, :])
    chain.link(dve, ins)
    rsqrt(nc, dve, chain, rv[:, 0:n], mv[:, 0:n, 1], rt[:, 0:n], rv[:, 0:n].bitcast(I32), mv[:, 0:n, 1].bitcast(I32), 0.0, EPS)
    for t in range(n):
        ins = nc.vector.tensor_scalar(dst[t], src[t], mv[:, t, 0:1], rv[:, t:t + 1], ALU.subtract, ALU.mult)
    chain.link(dve, ins)


LN_OPS = 3 + NEWTON_OPS


def batches(eng, body):
    for z in range(2):
        body(z, z, 0)
    with eng.Fori(1, B // 2) as m:
        for z in range(2):
            body(m * 2 + z, z, m)


def column(v):
    return v.rearrange("(p a) -> p a", a=1)


def load_constants(nc, bufs, bank, sem, ap):
    ident, identb, wa, wb, wc, wsrc, wtgt, wout = (bufs[k] for k in "ident identb wa wb wc wsrc wtgt wout".split())
    cols, loaded, made, turned, kept = bufs["cols"], sem("c_loaded"), sem("c_made"), sem("c_turned"), sem("c_kept")
    loads = [(wa["raw"], ap["Wa_w"]), (wb["raw"], ap["WB_w"]), (wc["raw"], ap["WC_w"]),
             (wsrc["raw"], ap["W_src"].rearrange("(a p) f -> p a f", p=P)), (wtgt["raw"], ap["W_tgt"]),
             (wout["raw"], ap["W_out"])]
    loads += cols
    with nc.Block() as block:

        @block.sync
        def _(sp):
            for dst, src in loads:
                sp.dma_start(dst, src, allow_slow_non_contiguous=True).then_inc(loaded, 16)
            sp.wait_ge(loaded, 16 * len(loads))

        @block.gpsimd
        def _(pool):
            nc.gpsimd.memset(ident, 0.0).then_inc(made, 1)
            pool.wait_ge(made, 1)
            nc.gpsimd.affine_select(out=ident, in_=ident, compare_op=ALU.not_equal, fill=1.0, base=0,
                                    pattern=[[-1, P]], channel_multiplier=1).then_inc(made, 1)
            pool.wait_ge(made, 2)
            nc.gpsimd.memset(bufs["zero_col"], 0.0).then_inc(made, 1)
            pool.wait_ge(made, 3)
            nc.gpsimd.memset(bufs["v_pad"], 0.0).then_inc(made, 1)
            pool.wait_ge(made, 4)
            nc.gpsimd.memset(bufs["minus_two"], -2.0).then_inc(made, 1)

        @block.tensor
        def _(pe):
            pe.wait_ge(loaded, 16 * len(loads))
            pe.wait_ge(made, 2)
            nc.tensor.transpose(bank[0][:, 0:ST], wa["raw"], ident[0:ST, 0:ST])
            nc.tensor.transpose(bank[0][:, ST:2 * ST], wb["raw"], ident[0:ST, 0:ST])
            nc.tensor.transpose(bank[0][:, P:2 * P], wtgt["raw"], ident)
            for f in range(2):
                nc.tensor.transpose(bank[0][:, (2 + f) * P:(3 + f) * P], wout["raw"][:, f * P:(f + 1) * P], ident)
            for f in range(2):
                for a in range(2):
                    nc.tensor.transpose(bank[1][:, (2 * f + a) * P:(2 * f + a + 1) * P], wsrc["raw"][:, a, f * P:(f + 1) * P], ident)
            nc.tensor.transpose(bank[2][0:ST, 0:P], wc["raw"], ident).then_inc(turned, 1)

        @block.vector
        def _(dve):
            dve.wait_ge(turned, 1)
            nc.vector.tensor_copy(wa["t"], bank[0][:, 0:ST])
            nc.vector.tensor_copy(wb["t"], bank[0][:, ST:2 * ST])
            nc.vector.tensor_copy(wtgt["t"], bank[0][:, P:2 * P])
            nc.vector.tensor_copy(wout["t"], bank[0][:, 2 * P:].rearrange("p (f o) -> p f o", o=P))
            nc.vector.tensor_copy(wsrc["t"], bank[1][:, :].rearrange("p (f o) -> p f o", o=2 * P))
            nc.vector.tensor_copy(wc["t"], bank[2][0:ST, 0:P])
            dve.wait_ge(made, 2)
            nc.vector.tensor_copy(identb, ident).then_inc(kept, 1)


def recurrence_inputs(nc, sb, sem, ap, bank, bufs, XR, XI, aS, uS):
    ident = bufs["ident"]
    xt = [sb(f"x_tok{z}", [P, NT, D]) for z in range(2)]
    xi = [sb(f"xin_tok{z}", [P, NT, D]) for z in range(2)]
    xn = [sb(f"xn_tok{z}", [P, NT, D]) for z in range(2)]
    xnT = [sb(f"xnT_{z}", [P, T]) for z in range(2)]
    st, mv, rv, rt = sb("st1", [P, NT, 6]), sb("mv1", [P, NT, 2]), sb("rv1", [P, NT]), sb("rt1", [P, NT])
    loaded = [Count(sem(f"x_loaded{z}"), 16) for z in range(2)]
    chain = Chain(sem("chain_in"), 2 * LN_OPS, bufs["passed"])
    turned = Count(sem("x_turned"), 2)
    kept = Count(sem("xT_kept"), 3)
    proj = Count(sem("au_done"), 1)
    au = Count(sem("au_kept"), 2)

    with nc.Block() as block:

        @block.sync
        def _(sp):
            def body(b, z, m):
                sp.wait_ge(turned.sem, turned.at(b - 1, 0))
                sp.dma_start(xt[z][:, :, :], ap["x"][b].rearrange("(t p) d -> p t d", p=P)).then_inc(loaded[z].sem, 16)

            for z in range(2):
                sp.dma_start(xt[z][:, :, :], ap["x"][z].rearrange("(t p) d -> p t d", p=P)).then_inc(loaded[z].sem, 16)
            with sp.Fori(1, B // 2) as m:
                for z in range(2):
                    body(m * 2 + z, z, m)

        @block.vector
        def _(dve):
            def body(b, z, m):
                dve.wait_ge(loaded[z].sem, loaded[z].at(m, 16))
                dve.wait_ge(turned.sem, turned.at(b, 0))
                chain.begin(b)
                layer_norm_tokens(nc, dve, chain, [xt[z][:, t, :] for t in range(NT)], [xi[z][:, t, :] for t in range(NT)], st, mv, rv, rt)
                layer_norm_tokens(nc, dve, chain, [xi[z][:, t, :] for t in range(NT)], [xn[z][:, t, :] for t in range(NT)], st, mv, rv, rt)
                dve.wait_ge(au.sem, au.at(b, 1))
                nc.vector.tensor_scalar(uS[:, b, :], bank[4 + z][0:ST, T:2 * T], bufs["WB_b"], None, ALU.add).then_inc(au.sem, 1)
            batches(dve, body)

        @block.tensor
        def _(pe):
            def body(b, z, m):
                chain_value = b * (2 * LN_OPS) + 2 * LN_OPS
                pe.wait_ge(chain.sem, chain_value)
                pe.wait_ge(kept.sem, kept.at(b, 0))
                for t in range(NT):
                    nc.tensor.transpose(bank[z][:, t * P:(t + 1) * P], xt[z][:, t, :], ident)
                for t in range(NT):
                    mm = nc.tensor.transpose(bank[z][:, T + t * P:T + (t + 1) * P], xi[z][:, t, :], ident)
                mm.then_inc(turned.sem, 1)
                for t in range(NT):
                    mm = nc.tensor.transpose(bank[2 + z][:, t * P:(t + 1) * P], xn[z][:, t, :], ident)
                mm.then_inc(turned.sem, 1)
                pe.wait_ge(kept.sem, kept.at(b, 3))
                pe.wait_ge(au.sem, au.at(b, 0))
                nc.tensor.matmul(bank[4 + z][0:ST, 0:T], bufs["wa"]["t"], xnT[z][:, :], start=True, stop=True)
                nc.tensor.matmul(bank[4 + z][0:ST, T:2 * T], bufs["wb"]["t"], xnT[z][:, :], start=True, stop=True).then_inc(proj.sem, 1)
            batches(pe, body)

        @block.scalar
        def _(act):
            def body(b, z, m):
                act.wait_ge(turned.sem, turned.at(b, 1))
                nc.scalar.activation(XR[:, b, :], bank[z][:, 0:T], ACT.Copy).then_inc(kept.sem, 1)
                nc.scalar.activation(XI[:, b, :], bank[z][:, T:2 * T], ACT.Copy).then_inc(kept.sem, 1)
                act.wait_ge(turned.sem, turned.at(b, 2))
                nc.scalar.activation(xnT[z][:, :], bank[2 + z][:, 0:T], ACT.Identity, scale=bufs["ln_w1"], bias=bufs["ln_b1"]).then_inc(kept.sem, 1)
                act.wait_ge(proj.sem, proj.at(b, 1))
                nc.scalar.activation(aS[:, b, :], bank[4 + z][0:ST, 0:T], ACT.Tanh, bias=bufs["Wa_b"]).then_inc(au.sem, 1)
            batches(act, body)


def recurrence(nc, sb, sem, ap, bank, bufs, XR, XI, aS, uS):
    R2 = 2 * B
    fre, fim, frr = sb("dft_re", [ST, 2 * P - SLOT]), sb("dft_im", [ST, 2 * P - SLOT]), sb("dft_real", [ST, 2 * R2 - 2])
    gre, gim, grr = sb("idft_re", [P, B, ST]), sb("idft_im", [P, B, ST]), sb("idft_real", [R2, B, ST])
    M = sb("a_u_planes", [P, 4, T])
    R = sb("a_u_real", [R2, 2, T])
    HR = sb("h_real", [R2, T])
    sqm = sb("sq_mag", [P, 2, T])
    mag = sb("mag", [P, T])
    gate = sb("gate", [P, T])
    mag_r, gate_r = sb("mag_r", [R2, T]), sb("gate_r", [R2, T])
    t1, t2 = sb("scan_t1", [P, 4, T]), sb("scan_t2", [P, 4, T])
    hT = sb("hT", [ST, B * T])
    gam = sb("gamma", [ST, 1])
    loaded, chain, achain = sem("dft_loaded"), Chain(sem("chain_scan")), Chain(sem("chain_gate_act"))
    gdone, dft, hs, inv, hk, yd = sem("gamma_done"), sem("dft_done"), sem("h_done"), sem("idft_done"), sem("hT_kept"), sem("y_done")
    marks = {}
    XRf, XIf = XR.rearrange("p b t -> p (b t)"), XI.rearrange("p b t -> p (b t)")
    LEVELS = [1 << k for k in range(T.bit_length() - 1)]
    tabs = [(fre, "c_dft_re"), (fim, "c_dft_im"), (frr, "c_dft_real"), (gre, "c_idft_re"), (gim, "c_idft_im"), (grr, "c_idft_real")]

    with nc.Block() as block:

        @block.sync
        def _(sp):
            for dst, name in tabs:
                sp.dma_start(dst[tuple([slice(None)] * len(dst.shape))], ap[name]).then_inc(loaded, 16)

        @block.scalar
        def _(act):
            nc.scalar.activation(gam[:, :], bufs["log_gamma"], ACT.Exp, scale=-1.0).then_inc(gdone, 1)
            act.wait_ge(dft, 1)
            achain.begin(0)
            nc.scalar.activation(sqm[:, :, :], bank[0][:, :].rearrange("p (a t) -> p a t", a=2), ACT.Square).then_inc(achain.sem, 1)
            nc.scalar.activation(mag_r[:, :], bank[2][0:R2, 0:T], ACT.Square).then_inc(achain.sem, 1)
            nc.scalar.activation(M[:, 2:4, :], bank[1][:, :].rearrange("p (a t) -> p a t", a=2), ACT.Copy).then_inc(achain.sem, 1)
            nc.scalar.activation(R[:, 1, :], bank[2][0:R2, T:2 * T], ACT.Copy).then_inc(achain.sem, 1)
            act.wait_ge(chain.sem, 5)
            nc.scalar.activation(mag[:, :], mag[:, :], ACT.Sqrt).then_inc(achain.sem, 1)
            nc.scalar.activation(mag_r[:, :], mag_r[:, :], ACT.Sqrt).then_inc(achain.sem, 1)
            act.wait_ge(achain.sem, 6)
            nc.scalar.activation(gate[:, :], mag[:, :], ACT.Exp, scale=2.0, bias=bufs["minus_two"]).then_inc(achain.sem, 1)
            nc.scalar.activation(gate_r[:, :], mag_r[:, :], ACT.Exp, scale=2.0, bias=bufs["minus_two"][0:R2, :]).then_inc(achain.sem, 1)
            for c in range(4):
                act.wait_ge(inv, c + 1)
                nc.scalar.activation(hT[:, c * CH:(c + 1) * CH], bank[3 + c][0:ST, :], ACT.Copy).then_inc(hk, 1)

        @block.tensor
        def _(pe):
            pe.wait_ge(loaded, 16 * len(tabs))
            pe.wait_ge(gdone, 2)
            for o, f, src in ((bank[0][:, 0:T], fre, aS), (bank[0][:, T:2 * T], fim, aS), (bank[1][:, 0:T], fre, uS),
                              (bank[1][:, T:2 * T], fim, uS)):
                for b in range(B):
                    lo = P - SLOT - SLOT * b
                    mm = nc.tensor.matmul(o, f[:, lo:lo + P], src[:, b, :], start=(b == 0), stop=(b == B - 1))
            for o, src in ((bank[2][0:R2, 0:T], aS), (bank[2][0:R2, T:2 * T], uS)):
                for b in range(B):
                    lo = R2 - 2 - 2 * b
                    mm = nc.tensor.matmul(o, frr[:, lo:lo + R2], src[:, b, :], start=(b == 0), stop=(b == B - 1))
            mm.then_inc(dft, 1)
            pe.wait_ge(hs, 2)
            for b in range(B):
                o = bank[3 + b // 2][0:ST, (b % 2) * T:(b % 2 + 1) * T]
                nc.tensor.matmul(o, gre[:, b, :], M[:, 2, :], start=True, stop=False)
                nc.tensor.matmul(o, gim[:, b, :], M[:, 3, :], start=False, stop=False)
                mm = nc.tensor.matmul(o, grr[:, b, :], HR[:, :], start=False, stop=True)
                if b % 2:
                    mm.then_inc(inv, 1)
            for c in range(4):
                pe.wait_ge(hk, c + 1)
                nc.tensor.matmul(bank[c][:, :] if c < 3 else bank[7][:, :], bufs["wc"]["t"], hT[:, c * CH:(c + 1) * CH],
                                 start=True, stop=True).then_inc(yd, 1)

        @block.vector
        def _(dve):
            dve.wait_ge(gdone, 1)
            chain.begin(0)
            chain.link(dve, nc.vector.tensor_scalar(gam[:, :], gam[:, :], 1.0, None, ALU.add))
            chain.link(dve, nc.vector.reciprocal(gam[:, :], gam[:, :]))
            nc.vector.tensor_scalar(aS, aS, gam[:, 0:1], None, ALU.mult).then_inc(gdone, 1)
            dve.wait_ge(achain.sem, 2)
            chain.link(dve, nc.vector.tensor_tensor(mag[:, :], sqm[:, 0, :], sqm[:, 1, :], ALU.add))
            chain.link(dve, nc.vector.tensor_scalar(mag[:, :], mag[:, :], 1e-16, None, ALU.max))
            chain.link(dve, nc.vector.tensor_scalar(mag_r[:, :], mag_r[:, :], 1e-16, None, ALU.max))
            dve.wait_ge(achain.sem, 8)
            for g_ in (gate, gate_r):
                chain.link(dve, nc.vector.tensor_scalar(g_[:, :], g_[:, :], 1.0, None, ALU.add))
                chain.link(dve, nc.vector.reciprocal(g_[:, :], g_[:, :]))
            chain.link(dve, nc.vector.tensor_tensor(M[:, 0:2, :], bank[0][:, :].rearrange("p (a t) -> p a t", a=2),
                                                    gate[:, :].unsqueeze(1).broadcast_to([P, 2, T]), ALU.mult))
            chain.link(dve, nc.vector.tensor_tensor(R[:, 0, :], bank[2][0:R2, 0:T], gate_r[:, :], ALU.mult))
            nc.vector.tensor_tensor_scan(HR[:, :], R[:, 0, :], R[:, 1, :], 0.0, ALU.mult, ALU.add).then_inc(hs, 1)
            for d in LEVELS:
                last = d == LEVELS[-1]
                pl = slice(2, 4) if last else slice(0, 4)
                np_, n = (2, T - d) if last else (4, T - d)
                for tt, plane in ((t1, 0), (t2, 1)):
                    chain.link(dve, nc.vector.tensor_tensor(tt[:, pl, 0:n], M[:, pl, 0:n],
                                                            M[:, plane, d:].unsqueeze(1).broadcast_to([P, np_, n]), ALU.mult))
                if not last:
                    chain.link(dve, nc.vector.tensor_tensor(M[:, 0, d:], t1[:, 0, 0:n], t2[:, 1, 0:n], ALU.subtract))
                    chain.link(dve, nc.vector.tensor_tensor(M[:, 1, d:], t1[:, 1, 0:n], t2[:, 0, 0:n], ALU.add))
                chain.link(dve, nc.vector.tensor_tensor(t1[:, 2, 0:n], t1[:, 2, 0:n], t2[:, 3, 0:n], ALU.subtract))
                chain.link(dve, nc.vector.tensor_tensor(t1[:, 3, 0:n], t1[:, 3, 0:n], t2[:, 2, 0:n], ALU.add))
                chain.link(dve, nc.vector.tensor_tensor(M[:, 2:4, d:], M[:, 2:4, d:], t1[:, 2:4, 0:n], ALU.add))
            nc.vector.tensor_copy(gam[:, :], gam[:, :]).then_inc(hs, 1)
            for c in range(4):
                x = XRf[:, c * CH:(c + 1) * CH]
                dve.wait_ge(yd, c + 1)
                chain.link(dve, nc.vector.scalar_tensor_tensor(x, (bank[c] if c < 3 else bank[7])[:, :], bufs["WC_b"], x, ALU.add, ALU.add))
                chain.link(dve, nc.vector.scalar_tensor_tensor(x, XIf[:, c * CH:(c + 1) * CH], bufs["D_skip"], x, ALU.mult, ALU.add))


def cross_attention(nc, sb, sem, ap, bank, bufs, XR, XT):
    ident, identb = bufs["ident"], bufs["identb"]
    ctx = [sb(f"ctx_tok{z}", [P, NT, CF]) for z in range(2)]
    mrow = [sb(f"mask_rows{z}", [P, S]) for z in range(2)]
    mcol = [sb(f"mask_cols{z}", [P, NT]) for z in range(2)]
    x2 = sb("x2", [P, T])
    x3 = sb("x3", [P, T])
    tn = sb("tgt_tok", [P, NT, D])
    tg = sb("tgtT", [P, T])
    cT = sb("ctxT", [P, 2, S])
    q = sb("q_x", [P, T])
    k = sb("k_x", [P, S])
    kh = sb("k_heads", [P, XH, S])
    mb = sb("mask_bias", [P, S], BF16)
    v = sb("v_x", [P, NT, D])
    vp = bufs["v_pad"]
    pr = [sb(f"pr{t}", [P, XH, S]) for t in range(NT)]
    mx, nm, sm = sb("mx_x", [P, NT, XH]), sb("nm_x", [P, NT, XH]), sb("sm_x", [P, NT, XH])
    pT = [sb(f"prT{t}", [P, XH, 2, P]) for t in range(NT)]
    up = sb("updT", [P, T])
    st, mv, rv, rt = sb("st2", [P, NT, 6]), sb("mv2", [P, NT, 2]), sb("rv2", [P, NT]), sb("rt2", [P, NT])
    sc, pt, pvb, ms = bank[0:4], bank[4:6], bank[6], bank[7]
    c_loaded = [Count(sem(f"ctx_loaded{z}"), 16 * 4) for z in range(2)]
    pe_ms = Count(sem("misc_done"), 10)
    x2c = Count(sem("x2_copied"), 1)
    chain = Chain(sem("chain_x"), 0, bufs["passed"])
    a_ms = Count(sem("misc_kept_act"), 4)
    v_ms = Count(sem("misc_kept_dve"), 6)
    scd = Count(sem("scores_x"), 8)
    mxd = Count(sem("max_x"), 8)
    exd = Count(sem("exp_x"), 8 * 2)
    nmd = Count(sem("norm_x"), 2)
    ptd = Count(sem("probs_turned_x"), 8)
    ptk = Count(sem("probT_kept_x"), 8)
    pvd = Count(sem("pv_x"), 2)
    upk = Count(sem("upd_kept"), 2)
    CH_OPS = 2 * LN_OPS + 14
    chain.per = CH_OPS

    with nc.Block() as block:

        @block.sync
        def _(sp):
            def load(b, z):
                s = c_loaded[z].sem
                sp.dma_start(ctx[z][:, :, :], ap["ctx"][b].rearrange("(t p) f -> p t f", p=P)).then_inc(s, 16)
                m = ap["mask"][b]
                sp.dma_start(mrow[z][:, :], m.rearrange("(a n) -> a n", a=1).broadcast_to([P, S])).then_inc(s, 16)
                for t in range(NT):
                    sp.dma_start(mcol[z][:, t:t + 1], column(m[t * P:(t + 1) * P]), allow_slow_non_contiguous=True).then_inc(s, 16)
            for z in range(2):
                load(z, z)
            with sp.Fori(1, B // 2) as m:
                for z in range(2):
                    sp.wait_ge(v_ms.sem, v_ms.at(m * 2 + z - 2, 6))
                    load(m * 2 + z, z)

        @block.tensor
        def _(pe):
            def body(b, z, m):
                pe.wait_ge(x2c.sem, x2c.at(b, 1))
                pe.wait_ge(a_ms.sem, a_ms.at(b, 0))
                for t in range(NT):
                    mm = nc.tensor.transpose(ms[:, t * P:(t + 1) * P], x2[:, t * P:(t + 1) * P], ident)
                mm.then_inc(pe_ms.sem, 1)
                pe.wait_ge(c_loaded[z].sem, c_loaded[z].at(m, 64))
                pe.wait_ge(exd.sem, exd.at(b, 0))
                for f in range(2):
                    for t in range(NT):
                        mm = nc.tensor.transpose(sc[0][:, f * S + t * P:f * S + (t + 1) * P], ctx[z][:, t, f * P:(f + 1) * P], ident)
                mm.then_inc(pe_ms.sem, 1)
                pe.wait_ge(a_ms.sem, a_ms.at(b, 1))
                for f in range(2):
                    mm = nc.tensor.matmul(sc[1][:, 0:S], bufs["wsrc"]["t"][:, f, 0:P], cT[:, f, :], start=(f == 0), stop=(f == 1))
                mm.then_inc(pe_ms.sem, 1)
                for t in range(NT):
                    for f in range(2):
                        mm = nc.tensor.matmul(sc[2][:, t * P:(t + 1) * P], cT[:, f, t * P:(t + 1) * P],
                                              bufs["wsrc"]["t"][:, f, P:2 * P], start=(f == 0), stop=(f == 1))
                mm.then_inc(pe_ms.sem, 1)
                pe.wait_ge(v_ms.sem, v_ms.at(b, 1))
                for t in range(NT):
                    mm = nc.tensor.transpose(ms[:, t * P:(t + 1) * P], tn[:, t, :], ident)
                mm.then_inc(pe_ms.sem, 1)
                pe.wait_ge(a_ms.sem, a_ms.at(b, 2))
                nc.tensor.matmul(sc[3][:, 0:T], bufs["wtgt"]["t"], tg[:, :], start=True, stop=True).then_inc(pe_ms.sem, 1)
                for t in range(NT):
                    for h in range(4):
                        if t == 0 and h == 0:
                            pe.wait_ge(v_ms.sem, v_ms.at(b, 4))
                        if t == 1:
                            pe.wait_ge(exd.sem, exd.at(b, 2 * h + 2))
                        nc.tensor.matmul(sc[h][:, :], identb, mb[:, :].unsqueeze(1).broadcast_to([P, 2, S]), start=True, stop=False)
                        nc.tensor.matmul(sc[h][:, :], q[:, t * P:(t + 1) * P], kh[:, 2 * h:2 * h + 2, :].rearrange("p h s -> p (h s)"),
                                         start=False, stop=True).then_inc(scd.sem, 1)
                for t in range(NT):
                    pe.wait_ge(nmd.sem, nmd.at(b, t + 1))
                    for h in range(4):
                        pe.wait_ge(ptk.sem, ptk.at(b, max(4 * t + h - 1, 0)))
                        for a in range(2):
                            for s in range(2):
                                mm = nc.tensor.transpose(pt[h % 2][:, (2 * a + s) * P:(2 * a + s + 1) * P],
                                                         pr[t][:, 2 * h + a, s * P:(s + 1) * P], ident)
                        mm.then_inc(ptd.sem, 1)
                    pe.wait_ge(ptk.sem, ptk.at(b, 4 * t + 4))
                    if t == 0:
                        pe.wait_ge(upk.sem, upk.at(b, 0))
                    for a in range(2):
                        for s in range(2):
                            for j in range(4):
                                mm = nc.tensor.matmul(pvb[32 * j:32 * j + 32, t * P:(t + 1) * P], vp[:, s, a, 32 * j:32 * j + 32],
                                                      pT[t][:, 2 * j + a, s, :], start=(a == 0 and s == 0), stop=(a == 1 and s == 1),
                                                      skip_group_check=True)
                    mm.then_inc(pvd.sem, 1)
                pe.wait_ge(upk.sem, upk.at(b, 2))
                nc.tensor.matmul(ms[:, 0:T], bufs["wout"]["t"][:, 0, :], tg[:, :], start=True, stop=False)
                nc.tensor.matmul(ms[:, 0:T], bufs["wout"]["t"][:, 1, :], up[:, :], start=False, stop=True).then_inc(pe_ms.sem, 1)
                pe.wait_ge(v_ms.sem, v_ms.at(b, 5))
                for t in range(NT):
                    mm = nc.tensor.transpose(ms[:, t * P:(t + 1) * P], x3[:, t * P:(t + 1) * P], ident)
                mm.then_inc(pe_ms.sem, 1)
                pe.wait_ge(v_ms.sem, v_ms.at(b, 6))
                for t in range(NT):
                    mm = nc.tensor.transpose(ms[:, T + t * P:T + (t + 1) * P], tn[:, t, :], ident)
                mm.then_inc(pe_ms.sem, 2)
            batches(pe, body)

        @block.scalar
        def _(act):
            def body(b, z, m):
                act.wait_ge(pe_ms.sem, pe_ms.at(b, 2))
                nc.scalar.activation(cT[:, :, :], sc[0][:, :].rearrange("p (f s) -> p f s", f=2), ACT.Copy).then_inc(a_ms.sem, 1)
                act.wait_ge(pe_ms.sem, pe_ms.at(b, 5))
                nc.scalar.activation(tg[:, :], ms[:, 0:T], ACT.Copy).then_inc(a_ms.sem, 1)
                for t in range(NT):
                    for h in range(4):
                        act.wait_ge(mxd.sem, mxd.at(b, 4 * t + h + 1))
                        for a in range(2):
                            n = 2 * h + a
                            nc.scalar.activation(pr[t][:, n, :], sc[h][:, a * S:(a + 1) * S], ACT.Exp, bias=nm[:, t, n:n + 1],
                                                 scale=float(XD) ** -0.5, accum_out=sm[:, t, n:n + 1]).then_inc(exd.sem, 1)
                for t in range(NT):
                    for h in range(4):
                        act.wait_ge(ptd.sem, ptd.at(b, 4 * t + h + 1))
                        nc.scalar.activation(pT[t][:, 2 * h:2 * h + 2, :, :], pt[h % 2][:, :].rearrange("p (h s t) -> p h s t", h=2, s=2),
                                             ACT.Copy).then_inc(ptk.sem, 1)
                    act.wait_ge(pvd.sem, pvd.at(b, t + 1))
                    nc.scalar.activation(up[:, t * P:(t + 1) * P], pvb[:, t * P:(t + 1) * P], ACT.Copy).then_inc(upk.sem, 1)
                act.wait_ge(pe_ms.sem, pe_ms.at(b, 10))
                nc.scalar.activation(XT[:, b, 1:1 + T], ms[:, T:2 * T], ACT.Copy).then_inc(a_ms.sem, 2)
            batches(act, body)

        @block.vector
        def _(dve):
            def body(b, z, m):
                chain.begin(b)
                link = lambda ins: chain.link(dve, ins)
                dve.wait_ge(pe_ms.sem, pe_ms.at(b, 0))
                dve.wait_ge(v_ms.sem, v_ms.at(b, 0))
                nc.vector.tensor_copy(x2[:, :], XR[:, b, :]).then_inc(x2c.sem, 1)
                dve.wait_ge(pe_ms.sem, pe_ms.at(b, 1))
                layer_norm_tokens(nc, dve, chain, [ms[:, t * P:(t + 1) * P] for t in range(NT)], [tn[:, t, :] for t in range(NT)], st, mv, rv, rt)
                nc.vector.tensor_copy(rt[:, 0:1], rv[:, 0:1]).then_inc(v_ms.sem, 1)
                dve.wait_ge(c_loaded[z].sem, c_loaded[z].at(m, 64))
                link(nc.vector.tensor_scalar(mb[:, :], mrow[z][:, :], 0.0, NEG, ALU.is_equal, ALU.mult))
                dve.wait_ge(pe_ms.sem, pe_ms.at(b, 3))
                link(nc.vector.scalar_tensor_tensor(k[:, :], sc[1][:, 0:S], bufs["b_k"], mrow[z][:, :], ALU.add, ALU.mult))
                for h in range(XH):
                    ins = nc.vector.tensor_scalar(kh[:, h, :], k[:, :], bufs["headmask"][:, h:h + 1], None, ALU.mult)
                    if h == XH - 1:
                        ins.then_inc(v_ms.sem, 1)
                dve.wait_ge(pe_ms.sem, pe_ms.at(b, 4))
                link(nc.vector.tensor_tensor(v[:, :, :], sc[2][:, 0:T].rearrange("p (t c) -> p t c", t=NT),
                                             bufs["b_v"].unsqueeze(1).broadcast_to([P, NT, D]), ALU.add))
                for t in range(NT):
                    for a in range(2):
                        ins = nc.vector.tensor_scalar(vp[:, t, a, :].rearrange("p (j a d) -> p j a d", a=2, d=XD)[:, :, a, :],
                                                      v[:, t, :].rearrange("p (j a d) -> p j a d", a=2, d=XD)[:, :, a, :],
                                                      mcol[z][:, t:t + 1], None, ALU.mult)
                ins.then_inc(v_ms.sem, 1)
                dve.wait_ge(pe_ms.sem, pe_ms.at(b, 6))
                nc.vector.scalar_tensor_tensor(q[:, :], sc[3][:, 0:T], bufs["b_q"], mrow[z][:, :], ALU.add, ALU.mult).then_inc(v_ms.sem, 1)
                for t in range(NT):
                    for h in range(4):
                        dve.wait_ge(scd.sem, scd.at(b, 4 * t + h + 1))
                        link(nc.vector.tensor_reduce(mx[:, t, 2 * h:2 * h + 2], sc[h][:, :].rearrange("p (a s) -> p a s", a=2), AX.X, ALU.max))
                        nc.vector.tensor_scalar(nm[:, t, 2 * h:2 * h + 2], mx[:, t, 2 * h:2 * h + 2], -float(XD) ** -0.5, None,
                                                ALU.mult).then_inc(mxd.sem, 1)
                for t in range(NT):
                    dve.wait_ge(exd.sem, exd.at(b, 8 * t + 8))
                    link(nc.vector.reciprocal(sm[:, t, :], sm[:, t, :]))
                    for h in range(XH):
                        ins = nc.vector.tensor_scalar(pr[t][:, h, :], pr[t][:, h, :], sm[:, t, h:h + 1], None, ALU.mult)
                    ins.then_inc(nmd.sem, 1)
                dve.wait_ge(pe_ms.sem, pe_ms.at(b, 7))
                link(nc.vector.scalar_tensor_tensor(x3[:, :], ms[:, 0:T], bufs["b_o"], x2[:, :], ALU.add, ALU.add))
                chain.apart(dve)
                nc.vector.tensor_copy(XR[:, b, :], x3[:, :]).then_inc(v_ms.sem, 1)
                dve.wait_ge(pe_ms.sem, pe_ms.at(b, 8))
                layer_norm_tokens(nc, dve, chain, [ms[:, t * P:(t + 1) * P] for t in range(NT)], [tn[:, t, :] for t in range(NT)], st, mv, rv, rt)
                nc.vector.tensor_copy(rt[:, 0:1], rv[:, 0:1]).then_inc(v_ms.sem, 1)
                assert chain.n == chain.per, chain.n
            batches(dve, body)


def output(nc, sb, sem, bank, ident, XR, XT, out):
    y = sb("y", [P, B, T])
    yo = sb("y_tok", [P, B, NT, D])
    summed, turned, kept, stored = sem("y_summed"), sem("y_turned"), sem("y_kept"), sem("y_stored")
    with nc.Block() as block:

        @block.vector
        def _(dve):
            for b in range(B):
                nc.vector.tensor_tensor(y[:, b, :], XR[:, b, :], XT[:, b, 1:1 + T], ALU.add).then_inc(summed, 1)

        @block.tensor
        def _(pe):
            for b in range(B):
                pe.wait_ge(summed, b + 1)
                for t in range(NT):
                    mm = nc.tensor.transpose(bank[b][:, t * P:(t + 1) * P], y[:, b, t * P:(t + 1) * P], ident)
                mm.then_inc(turned, 1)

        @block.scalar
        def _(act):
            for b in range(B):
                act.wait_ge(turned, b + 1)
                nc.scalar.activation(yo[:, b, :, :], bank[b][:, 0:T].rearrange("p (t d) -> p t d", t=NT), ACT.Copy).then_inc(kept, 1)

        @block.sync
        def _(sp):
            for b in range(B):
                sp.wait_ge(kept, b + 1)
                sp.dma_start(out[b].rearrange("(t p) d -> p t d", p=P), yo[:, b, :, :]).then_inc(stored, 16)
            sp.wait_ge(stored, 16 * B)


def decoder_block(nc, ap, out):
    with ExitStack() as ctx:
        def sb_in(stack):
            return lambda n, s, d=F32: stack.enter_context(nc.sbuf_tensor(n, s, d))

        sb = sb_in(ctx)
        sem = lambda n: ctx.enter_context(nc.semaphore(n))
        bank = [ctx.enter_context(nc.psum_tensor(f"bank{n}", [P, CH], F32)) for n in range(8)]
        XT = sb("x_layers", [P, B, 1 + T])
        XRt = sb("x_res", [P, B, T])
        XR = XRt[:, :, :]
        ident_t = sb("ident", [P, P])
        identb_t = sb("ident_bf", [P, P], BF16)
        passed = sem("waits_passed")
        with ExitStack() as first:
            sf = sb_in(first)
            vec = {n: sf(n + "_col", [r, 1]) for n, r in
                   (("Wa_b", ST), ("WB_b", ST), ("log_gamma", ST), ("ln_w1", P), ("ln_b1", P), ("WC_b", P), ("D_skip", P),
                    ("b_k", P), ("b_q", P), ("b_o", P))}
            src = {"ln_w1": ap["ln_w1"], "ln_b1": ap["ln_b1"], "b_k": ap["b_src"][0:P], "b_q": ap["b_tgt"], "b_o": ap["b_out"]}
            cols = []
            for n, t in vec.items():
                if n == "log_gamma":
                    cols.append((t[:, :], ap[n].rearrange("(a n) -> a n", a=1).broadcast_to([ST, 1])))
                else:
                    cols.append((t[:, :], column(src.get(n, ap.get(n)))))
            bv, hm = sf("b_v", [P, D]), sf("headmask", [P, XH])
            cols.append((bv[:, :], ap["b_src"][P:2 * P].rearrange("(a n) -> a n", a=1).broadcast_to([P, D])))
            cols.append((hm[:, :], ap["c_headmask"]))
            two = sf("minus_two", [P, 1])
            vp = sf("v_pad", [P, NT, 2, D])
            bufs = {n: t[:, :] for n, t in vec.items()}
            bufs |= {"passed": passed, "ident": ident_t[:, :], "identb": identb_t[:, :], "b_v": bv[:, :], "headmask": hm[:, :], "minus_two": two[:, :],
                     "v_pad": vp[:, :, :, :], "zero_col": XT[:, :, 0:1], "cols": cols}

            def weight(n, raw, t):
                a, b = sf(n + "_raw", raw), sf(n + "_t", t)
                bufs[n] = {"raw": a[tuple([slice(None)] * len(raw))], "t": b[tuple([slice(None)] * len(t))]}
            weight("wa", [ST, D], [D, ST])
            weight("wb", [ST, D], [D, ST])
            weight("wc", [D, ST], [ST, D])
            weight("wsrc", [P, 2, CF], [P, 2, 2 * D])
            weight("wtgt", [P, D], [P, D])
            weight("wout", [P, 2 * D], [P, 2, D])
            load_constants(nc, bufs, bank, sem, ap)
            with ExitStack() as part:
                XI = sb_in(part)("x_in", [P, B, T])[:, :, :]
                aS, uS = sb_in(part)("a_states", [ST, B, T])[:, :, :], sb_in(part)("u_states", [ST, B, T])[:, :, :]
                with ExitStack() as p2:
                    recurrence_inputs(nc, sb_in(p2), sem, ap, bank, bufs, XR, XI, aS, uS)
                with ExitStack() as p2:
                    recurrence(nc, sb_in(p2), sem, ap, bank, bufs, XR, XI, aS, uS)
            with ExitStack() as part:
                cross_attention(nc, sb_in(part), sem, ap, bank, bufs, XR, XT)
        with ExitStack() as part:
            layer_stage(nc, sb_in(part), bank, ident_t, identb_t, passed, sem, ap, XT)
        with ExitStack() as part:
            output(nc, sb_in(part), sem, bank, ident_t[:, :], XR, XT, out)


_INS = {"x": "x", "ctx": "ctx_2048", "mask": "mask_BxS2_fk1", "Wa_w": "L0_attn_Wa_w", "Wa_b": "L0_attn_Wa_b",
        "log_gamma": "L0_attn_log_gamma", "WB_w": "L0_attn_WB_w", "WB_b": "L0_attn_WB_b", "WC_w": "L0_attn_WC_w",
        "WC_b": "L0_attn_WC_b", "D_skip": "L0_attn_D_skip", "ln_w1": "L0_attn_ln_w", "ln_b1": "L0_attn_ln_b",
        "W_src": "L0_xattn_W_src", "b_src": "L0_xattn_b_src", "W_tgt": "L0_xattn_W_tgt", "b_tgt": "L0_xattn_b_tgt",
        "W_out": "L0_xattn_W_out", "b_out": "L0_xattn_b_out", "Wqkv": "L0_ffn_Wqkv", "q_scale": "L0_ffn_q_scale",
        "k_scale": "L0_ffn_k_scale", "Wo": "L0_ffn_Wo", "ln_g": "L0_ffn_ln_g", "ln_b": "L0_ffn_ln_b", "W1": "L0_ffn_W1",
        "b1": "L0_ffn_b1", "W2": "L0_ffn_W2", "b2": "L0_ffn_b2"}


def _tables():
    import numpy as np

    f = np.float32
    half = np.arange(0, DH, 2) * 1.0
    ang = np.arange(T)[:, None] / 10000.0 ** (half / DH)[None, :]
    scale = ((half + 0.4 * DH) / (1.4 * DH))[None, :] ** ((np.arange(T) - T // 2) / (W // 2))[:, None]
    ang, scale = np.concatenate([ang, ang], -1), np.concatenate([scale, scale], -1)
    sign = np.concatenate([-np.ones(DH // 2), np.ones(DH // 2)])
    rotary = np.stack([np.stack([np.cos(ang) * s, np.sin(ang) * s * sign]) for s in (scale, 1 / scale)])
    n = np.arange(ST)
    turn = 2 * np.pi * np.outer(n, np.arange(SLOT)) / ST
    live = (np.arange(SLOT) > 0) * 1.0
    wide = np.zeros((2, ST, 2 * P - SLOT))
    wide[0, :, P - SLOT:P] = np.cos(turn) * live
    wide[1, :, P - SLOT:P] = -np.sin(turn) * live
    real = np.stack([np.ones(ST), (-1.0) ** n])
    rwide = np.zeros((ST, 4 * B - 2))
    rwide[:, 2 * B - 2:2 * B] = real.T
    back = np.zeros((2, B, SLOT, B, ST))
    rback = np.zeros((B, 2, B, ST))
    for b in range(B):
        back[0, b, :, b, :] = (np.cos(turn) * live).T * 2 / ST
        back[1, b, :, b, :] = -(np.sin(turn) * live).T * 2 / ST
        rback[b, :, b, :] = real / ST
    back = back.reshape(2, P, B, ST)
    head = (np.arange(P)[:, None] // XD == np.arange(XH)[None, :]) * 1.0
    out = {"rotary": rotary, "c_dft_re": wide[0], "c_dft_im": wide[1], "c_dft_real": rwide, "c_idft_re": back[0],
           "c_idft_im": back[1], "c_idft_real": rback.reshape(2 * B, B, ST), "c_headmask": head}
    return {k: np.ascontiguousarray(v.astype(f)) for k, v in out.items()}


def kernel(**inputs):
    import numpy as _np
    import concourse.bacc as _bacc
    from concourse.bass_utils import run_bass_kernel_spmd as _run

    nc = _bacc.Bacc("TRN2", target_bir_lowering=False, num_devices=1)
    arrays = {name: _np.ascontiguousarray(inputs[full]) for name, full in _INS.items()} | _tables()
    feed = {f"in_{name}_dram": a for name, a in arrays.items()}
    ap = {name: nc.dram_tensor(f"in_{name}_dram", a.shape, F32, kind="ExternalInput").ap() for name, a in arrays.items()}
    out = nc.dram_tensor("out_0_dram", (B, T, D), F32, kind="ExternalOutput").ap()
    decoder_block(nc, ap, out)
    r = _run(nc, [feed], core_ids=[0])
    return r.results[0]["out_0_dram"]
```

```python
from contextlib import ExitStack

import concourse.bass as bass
from concourse import mybir

F32 = mybir.dt.float32
F32R = mybir.dt.float32r
BF16 = mybir.dt.bfloat16
I32 = mybir.dt.int32
ALU = mybir.AluOpType
ACT = mybir.ActivationFunctionType
AX = mybir.AxisListType

P = 128
B = 8
T = 256
D = 128
NT = T // P
ST = 32
QUAD = P // ST
SLOT = ST // 2
CF = 256
XH = 8
XD = D // XH
S = 256
L = 6
H = 16
DH = 64
INNER = H * DH
G = INNER // P
W = 32
NW = T // W
QW = P // W
CH = 512
QKV = 3 * INNER
KEEP, SHIFT = slice(0, D // 2), slice(D // 2, D)
NCH = QKV // CH
STAGE = 4
FI = int(D * 4 * 2 / 3)
FK = [(0, 128), (128, 128), (256, FI - 256)]
QK_SCALE = 8.0
EPS = 1e-5
NEG = -1e30
RSQRT_MAGIC = float(0x5F3759DF)
NEWTON = 3
NEWTON_OPS = 2 + 3 * NEWTON
POOL_NEWTON_OPS = 3 + 4 * NEWTON - 1
MADE = 18


class Count:

    def __init__(self, sem, per):
        self.sem, self.per = sem, per

    def at(self, unit, n):
        v = unit * self.per + n
        return max(v, 0) if isinstance(v, int) else v


class Chain:

    def __init__(self, sem, per=0, passed=None):
        self.sem, self.per, self.n, self.passed = sem, per, 0, passed

    def begin(self, unit):
        self.unit, self.n = unit, 0

    def link(self, eng, ins):
        ins.then_inc(self.sem, 1)
        self.n += 1
        eng.wait_ge(self.sem, self.unit * self.per + self.n)

    def apart(self, eng):
        eng.sem_inc(self.passed, 1)


def rsqrt(nc, dve, chain, y, x, t, y_int, x_int, floor, add):
    chain.link(dve, nc.vector.tensor_scalar(x, x, floor, add, ALU.max, ALU.add))
    chain.link(dve, nc.vector.tensor_scalar(y_int, x_int, -0.5, RSQRT_MAGIC, ALU.mult, ALU.add))
    for _ in range(NEWTON):
        chain.link(dve, nc.vector.tensor_tensor(t, y, y, ALU.mult))
        chain.link(dve, nc.vector.scalar_tensor_tensor(t, t, -0.5, x, ALU.mult, ALU.mult))
        chain.link(dve, nc.vector.scalar_tensor_tensor(y, t, 1.5, y, ALU.add, ALU.mult))


def layer_stage(nc, sb, bank, ident, identb, passed, sem, ap, XT):
    wst = sb("w_stage", [P, STAGE, CH])
    wh = sb("w_hi", [P, NCH, CH], F32R)
    wl = sb("w_lo", [P, NCH, CH], F32R)
    wo = sb("w_o", [P, G, D])
    w1 = sb("w_1", [P, 2 * FI])
    w2 = sb("w_2", [P, len(FK), D])
    par_ln = sb("ln_params", [P, 2])
    par_b1 = sb("b1_cols", [P, 2, len(FK)])
    par_b2 = sb("b2_col", [P, 1])
    scales = sb("qk_scales", [P, 2, 2, DH])
    base = sb("rotary_base", [P, 2, 2, NT, DH])
    tab = sb("rotary_tables", [P, 2, 2, NT, DH])
    xh = sb("xs_hi", [P, T], F32R)
    xl = sb("xs_lo", [P, T], F32R)
    sq = sb("squares", [P, 2, CH])
    tc = sb("times_cos", [P, 2, CH])
    ts = sb("times_sin", [P, 2, CH])
    U = sb("rotated", [P, NT, 4, CH])
    ss = sb("sum_squares", [P, NT, 2 * H])
    rn = sb("inv_norm", [P, NT, 2 * H])
    nt_ = sb("newton_tmp", [P, 2 * H])
    nx = sb("minus_half_x", [P, 2 * H])
    c15 = sb("three_halves", [P, 2 * H])
    qT = [sb(f"qT{p}", [P, G, T]) for p in range(2)]
    kT = [sb(f"kT{p}", [P, G, W + T]) for p in range(2)]
    vn = sb("v_tokens", [P, NT, 2, CH])
    vw = [sb(f"v_windows{p}", [P, NW, CH]) for p in range(2)]
    prob = [sb(f"prob{t}", [P, G, 2, DH]) for t in range(NT)]
    mx = sb("row_max", [P, NT, 2, G])
    sm = sb("row_sum", [P, NT, G, 2])
    rs = sb("inv_sum", [P, NT, G, 2])
    pT = [sb(f"probT{t}", [P, G, P]) for t in range(NT)]
    oT = [sb(f"oT{p}", [P, G, T]) for p in range(2)]
    xs = sb("x_shifted", [P, 1 + T])
    st = sb("ln_stats", [P, NT, 6])
    mv = sb("ln_mean_var", [P, NT, 2])
    rv = sb("ln_rstd", [P, NT, 2])
    rt = sb("ln_tmp", [P, NT, 2])
    xn = sb("x_norm", [P, NT, D])
    xnT = sb("x_normT", [P, T])
    act_ = sb("ffn_hidden", [P, len(FK), T])
    maskb = sb("window_mask", [P, NT, DH], BF16)

    Dk, C, A, Bk, E = bank[0:2], bank[2], bank[3:5], bank[5:7], bank[7]
    HB = [E, C, E]

    def cnt(name, per):
        return Count(sem(name), per)

    const = sem("consts_loaded")
    made = sem("consts_made")
    wdma = [cnt(f"wqkv_chunk_loaded{c}", 16) for c in range(NCH)]
    whi = cnt("wqkv_hi", NCH)
    wlo = cnt("wqkv_lo", NCH)
    fdma = cnt("ffn_weights_loaded", 16 * 11)
    sdma = cnt("qk_scales_loaded", 16 * 6)
    tabs = cnt("rotary_tables_made", 4)
    xs_hi = cnt("xs_hi_made", 1)
    xs_lo = cnt("xs_lo_made", 1)
    proj = cnt("proj_done", 12)
    squared = cnt("squared", 8)
    summed = cnt("squares_summed", 8)
    rot = cnt("rotary_products", 8)
    added = cnt("rotary_added", 8)
    normed = cnt("inv_norm_made", 2)
    scaled = cnt("qk_normalised", 8)
    turned = cnt("qk_transposed", 8)
    kept = cnt("qkT_kept", 8)
    v_kept = cnt("v_kept", 4)
    v_spread = [cnt("v_spread_tile0", 16 * 16), cnt("v_spread_tile1", 16 * 14)]
    c1 = Chain(sem("chain_norms"), 2 * POOL_NEWTON_OPS, passed)
    scored = cnt("scores_done", 4)
    maxed = cnt("max_done", 4)
    shifted = cnt("max_taken_off", 4)
    exped = cnt("exp_done", 2)
    sumd = cnt("row_sums", 2)
    inved = cnt("inv_sums", 2)
    p_turned = cnt("probs_transposed", 4)
    p_kept = cnt("probT_kept", 4)
    pv = cnt("pv_done", 4)
    o_kept = cnt("out_normalised", 4)
    o_turned = cnt("out_transposed", 4)
    oT_kept = cnt("outT_kept", 4)
    wo_done = cnt("wo_done", 1)
    x1_made = cnt("x1_made", 2)
    lna = cnt("ln_tokens_done", 1)
    c3 = Chain(sem("chain_ln"), 2 + NEWTON_OPS, passed)
    xn_made = cnt("xn_made", 2)
    lnb = cnt("xnT_done", 1)
    xnT_kept = cnt("xnT_kept", 1)
    hid = cnt("hidden_done", 3)
    gated = cnt("gelu_done", 3)
    hact = cnt("hidden_gated", 3)
    w2_done = cnt("w2_done", 1)
    fin = cnt("layer_out", 2)

    wq_d, wo_d, w1_d, w2_d = ap["Wqkv"], ap["Wo"], ap["W1"], ap["W2"]
    qs_d = [ap["q_scale"], ap["k_scale"]]
    U1, L1 = KEEP, SHIFT

    def pairs_view(t):
        return t.rearrange("p (h a d) -> p h a d", a=2, d=DH // 2)

    ALL = (True, True, True)

    def units(eng, body, layer_start):
        layer_start(0)
        body(0, 0, 0, (True, False, False), True, 0, None)
        body(1, 1, 1, (True, True, False), True, None, None)
        body(2, 2, 0, ALL, True, None, 0)
        body(3, 3, 1, ALL, True, None, None)
        with eng.Fori(2, B // 2) as m:
            for p in range(2):
                body(m * 2 + p, m * 2 + p, p, ALL, True, None, None)
        with eng.Fori(1, L) as l:
            layer_start(l)
            body(l * B, 0, 0, ALL, False, l, None)
            body(l * B + 1, 1, 1, ALL, False, None, None)
            with eng.Fori(1, B // 2) as m:
                for p in range(2):
                    body(l * B + m * 2 + p, m * 2 + p, p, ALL, False, None, l if p == 0 else None)
        n = L * B
        body(n, 0, 0, (False, True, True), False, None, None)
        body(n + 1, 1, 1, (False, False, True), False, None, None)

    def nothing(l):
        pass

    with nc.Block() as block:

        @block.sync
        def _(sp):
            sp.dma_start(base[:, :, :, :, :], ap["rotary"].rearrange("q s (t p) d -> p q s t d", p=P)).then_inc(const, 16)

            def load_qkv_chunk(l, c):
                dst = wst[:, c % STAGE, :]
                if c < 4:
                    src = wq_d[l, :, c * CH:(c + 1) * CH]
                else:
                    src = wq_d[l, :, 2 * INNER:].rearrange("k (g a d) -> k a g d", a=2, d=DH)[:, c - 4, :, :]
                    dst = dst.rearrange("k (g d) -> k g d", d=DH)
                sp.dma_start(dst, src).then_inc(wdma[c].sem, 16)

            def load_ffn(l):
                sp.wait_ge(w2_done.sem, w2_done.at(l * B, 0))
                sp.sem_inc(passed, 1)
                sp.wait_ge(fin.sem, fin.at(l * B, 0))
                s = fdma.sem
                sp.dma_start(wo[:, :, :], wo_d[l].rearrange("(g p) n -> p g n", p=P)).then_inc(s, 16)
                sp.dma_start(w1[:, :], w1_d[l]).then_inc(s, 16)
                sp.dma_start(w2[:, 0:2, :], w2_d[l, 0:256, :].rearrange("(k p) n -> p k n", p=P)).then_inc(s, 16)
                sp.dma_start(w2[0:FK[2][1], 2, :], w2_d[l, 256:FI, :]).then_inc(s, 16)
                sp.dma_start(par_ln[:, 0:1], ap["ln_g"][l].rearrange("(p a) -> p a", a=1),
                             allow_slow_non_contiguous=True).then_inc(s, 16)
                sp.dma_start(par_ln[:, 1:2], ap["ln_b"][l].rearrange("(p a) -> p a", a=1),
                             allow_slow_non_contiguous=True).then_inc(s, 16)
                for a in range(2):
                    sp.dma_start(par_b1[:, a, 0:2], ap["b1"][l, a * FI:a * FI + 256].rearrange("(k p) -> p k", p=P),
                                 allow_slow_non_contiguous=True).then_inc(s, 16)
                    sp.dma_start(par_b1[0:FK[2][1], a, 2:3],
                                 ap["b1"][l, a * FI + 256:(a + 1) * FI].rearrange("(p a) -> p a", a=1),
                             allow_slow_non_contiguous=True).then_inc(s, 16)
                sp.dma_start(par_b2[:, :], ap["b2"][l].rearrange("(p a) -> p a", a=1),
                             allow_slow_non_contiguous=True).then_inc(s, 16)

            def load_first_chunks(l):
                sp.wait_ge(wlo.sem, wlo.at(l, 0))
                for c in range(STAGE):
                    load_qkv_chunk(l, c)

            def load_last_chunks(l):
                for c in range(STAGE, NCH):
                    sp.wait_ge(wlo.sem, wlo.at(l, c - STAGE + 1))
                    load_qkv_chunk(l, c)

            def load_scales(l):
                sp.wait_ge(tabs.sem, tabs.at(l, 0))
                for q in range(2):
                    row = qs_d[q][l].rearrange("(a n) -> a n", a=1)
                    sp.dma_start(scales[:, q, 0, :], row.broadcast_to([P, DH])).then_inc(sdma.sem, 16)
                    for a in range(2):
                        half = row[:, (1 - a) * 32:(2 - a) * 32]
                        sp.dma_start(scales[:, q, 1, a * 32:a * 32 + 32], half.broadcast_to([P, DH // 2])).then_inc(sdma.sem, 16)

            def spread_v(u, p, t):
                sp.wait_ge(v_kept.sem, v_kept.at(u, 2 * t + 2))
                sp.wait_ge(pv.sem, pv.at(u - 1, 0))
                for c in range(QW * t, QW * (t + 1)):
                    src = vn[W * (c % QW):W * (c % QW) + W, t, :, :]
                    for kb, w in ((1, c), (0, c + 1)):
                        if w == NW:
                            continue
                        for a in range(2):
                            row = 64 * a + W * kb
                            sp.dma_start(vw[p][row:row + W, w, :], src[:, a, :]).then_inc(v_spread[t].sem, 16)

            def body(i, p):
                for t in range(NT):
                    spread_v(i, p, t)

            def layer(l):
                load_last_chunks(l)
                for p in range(2):
                    body(l * B + p, p)
                load_ffn(l)
                load_first_chunks(l + 1)
                load_scales(l + 1)
                with sp.Fori(1, B // 2) as m:
                    for p in range(2):
                        body(l * B + m * 2 + p, p)

            load_first_chunks(0)
            load_scales(0)
            load_last_chunks(0)
            for p in range(2):
                body(p, p)
            load_ffn(0)
            load_first_chunks(1)
            load_scales(1)
            for p in range(2):
                body(2 + p, p)
            with sp.Fori(2, B // 2) as m:
                for p in range(2):
                    body(m * 2 + p, p)
            with sp.Fori(1, L - 1) as l:
                layer(l)
            last = L - 1
            load_last_chunks(last)
            for p in range(2):
                body(last * B + p, p)
            load_ffn(last)
            with sp.Fori(1, B // 2) as m:
                for p in range(2):
                    body(last * B + m * 2 + p, p)

        @block.gpsimd
        def _(pool):
            c = Chain(made)
            c.begin(0)

            def do(ins):
                c.link(pool, ins)

            do(nc.gpsimd.memset(c15[:, :], 1.5))
            do(nc.gpsimd.memset(xs[:, :], 0.0))
            for p in range(2):
                do(nc.gpsimd.memset(kT[p][:, :, 0:W], 0.0))
                for a in range(2):
                    do(nc.gpsimd.memset(vw[p][64 * a:64 * a + W, 0, :], 0.0))
            do(nc.gpsimd.memset(maskb[:, :, :], 0.0))
            for w in range(QW):
                rows = maskb[W * w:W * w + W, :, :]
                do(nc.gpsimd.affine_select(out=rows, in_=rows, compare_op=ALU.is_ge, fill=NEG, base=0,
                                           pattern=[[0, NT], [1, 2 * W]], channel_multiplier=-1))
                do(nc.gpsimd.affine_select(out=rows, in_=rows, compare_op=ALU.is_ge, fill=NEG, base=W,
                                           pattern=[[0, NT], [-1, 2 * W]], channel_multiplier=1))
            do(nc.gpsimd.memset(maskb[0:W, 0, 0:W], NEG))
            assert c.n == MADE
            pool.wait_ge(const, 16)

            def tables(l):
                pool.wait_ge(sdma.sem, sdma.at(l, 16 * 6))
                pool.wait_ge(rot.sem, rot.at(l * B, 0))
                for q in range(2):
                    for s in range(2):
                        sc = scales[:, q, s, :].unsqueeze(1).broadcast_to([P, NT, DH])
                        nc.gpsimd.tensor_tensor(tab[:, q, s, :, :], base[:, q, s, :, :], sc, ALU.mult).then_inc(tabs.sem, 1)

            def add(u, f):
                pool.wait_ge(rot.sem, rot.at(u, f + 1))
                pool.wait_ge(turned.sem, turned.at(u - 1, f + 1))
                nc.gpsimd.tensor_tensor(U[:, f // 4, f % 4, :], tc[:, f % 2, :], ts[:, f % 2, :], ALU.add).then_inc(added.sem, 1)

            def norm(u, f):
                t, c = f // 4, f % 4
                pool.wait_ge(normed.sem, normed.at(u, t + 1))
                pool.wait_ge(added.sem, added.at(u, f + 1))
                v = U[:, t, c, :].rearrange("p (h d) -> p h d", d=DH)
                r = rn[:, t, 8 * c:8 * c + 8].unsqueeze(2).broadcast_to([P, 8, DH])
                nc.gpsimd.tensor_tensor(v, v, r, ALU.mult).then_inc(scaled.sem, 1)

            def inv_norms(u, t):
                pool.wait_ge(summed.sem, summed.at(u, 4 * t + 4))
                c1.begin(u)
                c1.n = t * POOL_NEWTON_OPS
                c1.apart(pool)
                y, x, h, tmp = rn[:, t, :], ss[:, t, :], nx[:, :], nt_[:, :]
                c1.link(pool, nc.gpsimd.tensor_scalar(x, x, 1e-24, None, ALU.max))
                c1.apart(pool)
                c1.link(pool, nc.gpsimd.tensor_scalar(y.bitcast(I32), x.bitcast(I32), -0.5, RSQRT_MAGIC, ALU.mult, ALU.add))
                c1.apart(pool)
                c1.link(pool, nc.gpsimd.tensor_scalar(h, x, -0.5, None, ALU.mult))
                for step in range(NEWTON):
                    c1.link(pool, nc.gpsimd.tensor_tensor(tmp, y, y, ALU.mult))
                    c1.link(pool, nc.gpsimd.tensor_tensor(tmp, tmp, h, ALU.mult))
                    c1.link(pool, nc.gpsimd.tensor_tensor(tmp, tmp, c15[:, :], ALU.add))
                    if step < NEWTON - 1:
                        c1.link(pool, nc.gpsimd.tensor_tensor(y, y, tmp, ALU.mult))
                nc.gpsimd.tensor_tensor(y, y, tmp, ALU.mult).then_inc(normed.sem, 1)

            def body(i, j, p, on, layer0, new, ffn):
                s1, s2, s3 = on
                if s2:
                    inv_norms(i - 1, 1)
                    for f in range(4, 8):
                        norm(i - 1, f)
                if s1:
                    for f in range(4):
                        add(i, f)
                    inv_norms(i, 0)
                    for f in range(4):
                        norm(i, f)
                    for f in range(4, 8):
                        add(i, f)
            units(pool, body, tables)

        @block.scalar
        def _(act):
            act.wait_ge(made, MADE)

            def split_weights(l):
                act.wait_ge(proj.sem, proj.at(l * B, 0))
                for c in range(STAGE):
                    split_chunk(l, c)

            def split_chunk(l, c):
                act.wait_ge(wdma[c].sem, wdma[c].at(l, 16))
                nc.scalar.activation(wh[:, c, :], wst[:, c % STAGE, :], ACT.Copy).then_inc(whi.sem, 1)

            def x_hi(u, j, layer0):
                if not layer0:
                    act.wait_ge(fin.sem, fin.at(u - B, 2))
                act.wait_ge(proj.sem, proj.at(u, 0))
                nc.scalar.activation(xh[:, :], XT[:, j, 0:T], ACT.Copy).then_inc(xs_hi.sem, 1)

            def square(u, k):
                f = k // 6 * 4 + k % 6
                act.wait_ge(proj.sem, proj.at(u, k + 1))
                act.wait_ge(summed.sem, summed.at(u, f - 1))
                nc.scalar.activation(sq[:, f % 2, :], Dk[k % 2][:, :], ACT.Square).then_inc(squared.sem, 1)

            def keep_v(u, k):
                t, a = k // 6, k % 6 - 4
                act.wait_ge(proj.sem, proj.at(u, k + 1))
                act.wait_ge(v_spread[t].sem, v_spread[t].at(u, 0))
                nc.scalar.activation(vn[:, t, a, :], Dk[k % 2][:, :], ACT.Copy).then_inc(v_kept.sem, 1)

            def keep_qk(u, p, f):
                t, c = f // 4, f % 4
                act.wait_ge(turned.sem, turned.at(u, f + 1))
                act.wait_ge(scored.sem, scored.at(u - 1, 0))
                src = C[:, :].rearrange("p (g n) -> p g n", n=P)
                g = 4 * (c % 2)
                if c < 2:
                    dst = qT[p][:, g:g + 4, t * P:(t + 1) * P]
                else:
                    dst = kT[p][:, g:g + 4, W + t * P:W + (t + 1) * P]
                nc.scalar.activation(dst, src, ACT.Copy).then_inc(kept.sem, 1)

            def exp(u, t):
                act.wait_ge(shifted.sem, shifted.at(u, 2 * t + 2))
                nc.scalar.activation(prob[t][:, :, :, :], prob[t][:, :, :, :], ACT.Exp, scale=QK_SCALE).then_inc(exped.sem, 1)

            def keep_pT(u, t, h):
                act.wait_ge(p_turned.sem, p_turned.at(u, 2 * t + h + 1))
                act.wait_ge(pv.sem, pv.at(u - 1, 2 * t + 2))
                nc.scalar.activation(pT[t][:, 4 * h:4 * h + 4, :], Bk[h][:, :].rearrange("p (g n) -> p g n", n=P),
                                     ACT.Copy).then_inc(p_kept.sem, 1)

            def keep_oT(u, p, t, h):
                act.wait_ge(o_turned.sem, o_turned.at(u, 2 * t + h + 1))
                act.wait_ge(wo_done.sem, wo_done.at(u - 1, 0))
                nc.scalar.activation(oT[p][:, 4 * h:4 * h + 4, t * P:(t + 1) * P],
                                     Bk[h][:, :].rearrange("p (g n) -> p g n", n=P), ACT.Copy).then_inc(oT_kept.sem, 1)

            def keep_xnT(u):
                act.wait_ge(lnb.sem, lnb.at(u, 1))
                nc.scalar.activation(xnT[:, :], E[:, 0:T], ACT.Identity, scale=par_ln[:, 0:1],
                                     bias=par_ln[:, 1:2]).then_inc(xnT_kept.sem, 1)

            def gelu(u, k):
                m = FK[k][1]
                act.wait_ge(hid.sem, hid.at(u, k + 1))
                nc.scalar.activation(act_[0:m, k, :], HB[k][0:m, T:2 * T], ACT.Gelu, bias=par_b1[0:m, 1, k:k + 1]).then_inc(gated.sem, 1)

            def body(i, j, p, on, layer0, new, ffn):
                s1, s2, s3 = on
                a, b, q = i - 1, i - 2, 1 - p
                if s1:
                    x_hi(i, j, layer0)
                if s2:
                    keep_qk(a, q, 2)
                if s1:
                    square(i, 0)
                if s2:
                    keep_qk(a, q, 3)
                if s1:
                    square(i, 1)
                if s3:
                    keep_pT(b, 1, 0)
                    keep_pT(b, 1, 1)
                if new is not None:
                    for c in range(STAGE, NCH):
                        split_chunk(new, c)
                if s1:
                    square(i, 2)
                if s2:
                    exp(a, 0)
                if s1:
                    square(i, 3)
                if s2:
                    keep_qk(a, q, 4)
                if s1:
                    keep_v(i, 4)
                if s3:
                    keep_oT(b, p, 1, 0)
                    keep_oT(b, p, 1, 1)
                if s2:
                    keep_qk(a, q, 5)
                if s1:
                    keep_v(i, 5)
                    square(i, 6)
                if s2:
                    keep_qk(a, q, 6)
                    keep_pT(a, 0, 0)
                    keep_pT(a, 0, 1)
                    keep_qk(a, q, 7)
                if s1:
                    square(i, 7)
                if s3:
                    keep_xnT(b)
                if s1:
                    square(i, 8)
                if s2:
                    exp(a, 1)
                if s3:
                    gelu(b, 0)
                    gelu(b, 1)
                if s1:
                    square(i, 9)
                if s2:
                    keep_oT(a, q, 0, 0)
                    keep_oT(a, q, 0, 1)
                if s3:
                    gelu(b, 2)
                if s1:
                    keep_qk(i, p, 0)
                    keep_v(i, 10)
                    keep_qk(i, p, 1)
                    keep_v(i, 11)
            units(act, body, split_weights)

        @block.tensor
        def _(pe):
            pe.wait_ge(made, MADE)

            def project(u, k, new):
                t, c = k // 6, k % 6
                if k == 0:
                    pe.wait_ge(xs_lo.sem, xs_lo.at(u, 1))
                if new is not None and t == 0:
                    pe.wait_ge(wlo.sem, wlo.at(new, c + 1))
                kk, uu = (k - 2, u) if k >= 2 else (k + 10, u - 1)
                tt, cc = kk // 6, kk % 6
                if cc < 4:
                    pe.wait_ge(rot.sem, rot.at(uu, 4 * tt + cc + 1))
                else:
                    pe.wait_ge(v_kept.sem, v_kept.at(uu, 2 * tt + cc - 4 + 1))
                out = Dk[k % 2][:, :]
                tok = slice(t * P, (t + 1) * P)
                nc.tensor.matmul(out, xh[:, tok], wh[:, c, :], start=True, stop=False)
                nc.tensor.matmul(out, xh[:, tok], wl[:, c, :], start=False, stop=False)
                nc.tensor.matmul(out, xl[:, tok], wh[:, c, :], start=False, stop=True).then_inc(proj.sem, 1)

            def turn_qk(u, f, ffn_unit=None):
                t, c = f // 4, f % 4
                if ffn_unit is not None:
                    pe.wait_ge(hact.sem, hact.at(ffn_unit, 2))
                pe.wait_ge(scaled.sem, scaled.at(u, f + 1))
                pe.wait_ge(kept.sem, kept.at(u, f))
                for g in range(4):
                    mm = nc.tensor.transpose(C[:, g * P:(g + 1) * P], U[:, t, c, g * P:(g + 1) * P], ident[:, :])
                mm.then_inc(turned.sem, 1)

            def scores(u, p, t):
                pe.wait_ge(kept.sem, kept.at(u, 4 * (t + 1)))
                pe.wait_ge(shifted.sem, shifted.at(u, 2 * t))
                for a in range(2):
                    nc.tensor.matmul(A[a][:, :], identb[:, :], maskb[:, t, :].unsqueeze(1).broadcast_to([P, G, DH]),
                                     start=True, stop=False, skip_group_check=True)
                for g in range(G):
                    for w in range(QW):
                        for a in range(2):
                            row = 64 * a
                            col = t * P + W * w
                            mm = nc.tensor.matmul(A[a][W * w:W * w + W, g * DH:(g + 1) * DH],
                                                  qT[p][row:row + 64, g, col:col + W],
                                                  kT[p][row:row + 64, g, col:col + 2 * W],
                                                  start=False, stop=True, skip_group_check=True)
                            if g == G - 1 and w == QW - 1:
                                mm.then_inc(scored.sem, 1)

            def turn_p(u, t, h):
                pe.wait_ge(exped.sem, exped.at(u, t + 1))
                if t == 0:
                    pe.wait_ge(oT_kept.sem, oT_kept.at(u - 1, 2 + h + 1))
                else:
                    pe.wait_ge(oT_kept.sem, oT_kept.at(u, h + 1))
                for g in range(4):
                    mm = nc.tensor.transpose(Bk[h][:, g * P:(g + 1) * P],
                                             prob[t][:, 4 * h + g, :, :].rearrange("p a d -> p (a d)"), ident[:, :])
                mm.then_inc(p_turned.sem, 1)

            def values(u, p, t):
                pe.wait_ge(p_kept.sem, p_kept.at(u, 2 * t + 2))
                pe.wait_ge(v_spread[0].sem, v_spread[0].at(u, 16 * 16))
                if t:
                    pe.wait_ge(v_spread[1].sem, v_spread[1].at(u, 16 * 14))
                pe.sem_inc(passed, 1)
                for g in range(G):
                    for w in range(QW):
                        for a in range(2):
                            row = 64 * a
                            mm = nc.tensor.matmul(Bk[a][W * w:W * w + W, g * DH:(g + 1) * DH],
                                                  pT[t][row:row + 64, g, W * w:W * w + W],
                                                  vw[p][row:row + 64, QW * t + w, g * DH:(g + 1) * DH],
                                                  start=True, stop=True, skip_group_check=True)
                            if g == G - 1 and w == QW - 1:
                                mm.then_inc(pv.sem, 1)

            def turn_o(u, t, h):
                pe.wait_ge(o_kept.sem, o_kept.at(u, 2 * t + 2))
                pe.wait_ge(p_kept.sem, p_kept.at(u, 2 * t + h + 1))
                for g in range(4):
                    mm = nc.tensor.transpose(Bk[h][:, g * P:(g + 1) * P],
                                             prob[t][:, 4 * h + g, :, :].rearrange("p a d -> p (a d)"), ident[:, :])
                mm.then_inc(o_turned.sem, 1)

            def out_proj(u, p, ffn):
                if ffn is not None:
                    pe.wait_ge(fdma.sem, fdma.at(ffn, 16 * 11))
                pe.wait_ge(oT_kept.sem, oT_kept.at(u, 4))
                pe.wait_ge(fin.sem, fin.at(u, 0))
                for g in range(G):
                    mm = nc.tensor.matmul(E[:, 0:T], wo[:, g, :], oT[p][:, g, :], start=(g == 0), stop=(g == G - 1))
                mm.then_inc(wo_done.sem, 1)

            def ln_tokens(u):
                pe.wait_ge(x1_made.sem, x1_made.at(u, 2))
                for t in range(NT):
                    mm = nc.tensor.transpose(E[:, t * P:(t + 1) * P], xs[:, t * P:(t + 1) * P], ident[:, :])
                mm.then_inc(lna.sem, 1)

            def ln_back(u):
                pe.wait_ge(xn_made.sem, xn_made.at(u, 2))
                for t in range(NT):
                    mm = nc.tensor.transpose(E[:, t * P:(t + 1) * P], xn[:, t, :], ident[:, :])
                mm.then_inc(lnb.sem, 1)

            def hidden(u, k, turned_unit):
                o, m = FK[k]
                if k == 0:
                    pe.wait_ge(xnT_kept.sem, xnT_kept.at(u, 1))
                elif k == 1:
                    pe.wait_ge(kept.sem, kept.at(turned_unit, 8))
                else:
                    pe.wait_ge(hact.sem, hact.at(u, 1))
                nc.tensor.matmul(HB[k][0:m, 0:T], w1[:, o:o + m], xnT[:, :], start=True, stop=True)
                nc.tensor.matmul(HB[k][0:m, T:2 * T], w1[:, FI + o:FI + o + m], xnT[:, :], start=True, stop=True).then_inc(hid.sem, 1)

            def ffn_out(u):
                pe.wait_ge(hact.sem, hact.at(u, 3))
                for k, (o, m) in enumerate(FK):
                    mm = nc.tensor.matmul(E[:, 0:T], w2[0:m, k, :], act_[0:m, k, :], start=(k == 0), stop=(k == 2))
                mm.then_inc(w2_done.sem, 1)

            def body(i, j, p, on, layer0, new, ffn):
                s1, s2, s3 = on
                a, b, q = i - 1, i - 2, 1 - p
                if s1:
                    project(i, 0, new)
                if s2:
                    turn_qk(a, 3)
                if s1:
                    project(i, 1, new)
                if s3:
                    turn_p(b, 1, 0)
                    turn_p(b, 1, 1)
                if s2:
                    scores(a, q, 0)
                if s1:
                    project(i, 2, new)
                if s3:
                    values(b, p, 1)
                if s1:
                    project(i, 3, new)
                if s2:
                    turn_qk(a, 4)
                if s1:
                    project(i, 4, new)
                if s3:
                    turn_o(b, 1, 0)
                    turn_o(b, 1, 1)
                if s2:
                    turn_qk(a, 5)
                if s1:
                    project(i, 5, new)
                if s3:
                    out_proj(b, p, ffn)
                if s1:
                    project(i, 6, new)
                if s2:
                    turn_qk(a, 6)
                    turn_p(a, 0, 0)
                if s3:
                    ln_tokens(b)
                if s2:
                    turn_p(a, 0, 1)
                    turn_qk(a, 7)
                if s1:
                    project(i, 7, new)
                if s2:
                    scores(a, q, 1)
                if s3:
                    ln_back(b)
                if s1:
                    project(i, 8, new)
                if s2:
                    values(a, q, 0)
                if s3:
                    hidden(b, 0, None)
                    hidden(b, 1, a if s2 else b)
                if s1:
                    project(i, 9, new)
                if s2:
                    turn_o(a, 0, 0)
                    turn_o(a, 0, 1)
                if s3:
                    hidden(b, 2, None)
                if s1:
                    turn_qk(i, 0, b if s3 else None)
                    project(i, 10, new)
                    turn_qk(i, 1)
                    project(i, 11, new)
                if s3:
                    ffn_out(b)
                if s1:
                    turn_qk(i, 2)
            units(pe, body, nothing)

        @block.vector
        def _(dve):
            dve.wait_ge(made, MADE)

            def split_weights(l):
                for c in range(STAGE):
                    split_chunk(l, c)
                dve.wait_ge(tabs.sem, tabs.at(l, 4))

            def split_chunk(l, c):
                dve.wait_ge(whi.sem, whi.at(l, c + 1))
                nc.vector.tensor_tensor(wl[:, c, :], wst[:, c % STAGE, :], wh[:, c, :].bitcast(F32),
                                        ALU.subtract).then_inc(wlo.sem, 1)

            def x_lo(u, j):
                dve.wait_ge(xs_hi.sem, xs_hi.at(u, 1))
                nc.vector.tensor_tensor(xl[:, :], XT[:, j, 0:T], xh[:, :].bitcast(F32), ALU.subtract).then_inc(xs_lo.sem, 1)

            def rotate(u, k):
                t, c = k // 6, k % 6
                f = 4 * t + c
                q = c // 2
                dve.wait_ge(squared.sem, squared.at(u, f + 1))
                dve.wait_ge(added.sem, added.at(u, f - 1))
                cos = tab[:, q, 0, t, :].unsqueeze(1).broadcast_to([P, 8, DH])
                sin = tab[:, q, 1, t, :].rearrange("p (a d) -> p a d", a=2).unsqueeze(1).broadcast_to([P, 8, 2, DH // 2])
                nc.vector.tensor_tensor(tc[:, f % 2, :].rearrange("p (h d) -> p h d", d=DH),
                                        Dk[k % 2][:, :].rearrange("p (h d) -> p h d", d=DH), cos, ALU.mult)
                swapped = pairs_view(Dk[k % 2][:, :])[:, :, ::-1, :]
                nc.vector.tensor_tensor(pairs_view(ts[:, f % 2, :]), swapped, sin, ALU.mult).then_inc(rot.sem, 1)
                dve.wait_ge(normed.sem, normed.at(u - 1, t + 1))
                nc.vector.tensor_reduce(ss[:, t, 8 * c:8 * c + 8], sq[:, f % 2, :].rearrange("p (h d) -> p h d", d=DH),
                                        AX.X, ALU.add).then_inc(summed.sem, 1)

            def row_max(u, t, a):
                dve.wait_ge(scored.sem, scored.at(u, 2 * t + a + 1))
                src = A[a][:, :].rearrange("p (g d) -> p g d", d=DH)
                nc.vector.tensor_reduce(mx[:, t, a, :], src, AX.X, ALU.max).then_inc(maxed.sem, 1)

            def take_max(u, t, a):
                dve.wait_ge(maxed.sem, maxed.at(u, 2 * t + a + 1))
                if a == 0:
                    dve.wait_ge(o_turned.sem, o_turned.at(u - 1, 2 * t + 2))
                src = A[a][:, :].rearrange("p (g d) -> p g d", d=DH)
                nc.vector.tensor_tensor(prob[t][:, :, a, :], src, mx[:, t, a, :].unsqueeze(2).broadcast_to([P, G, DH]),
                                        ALU.subtract).then_inc(shifted.sem, 1)

            def row_sum(u, t):
                dve.wait_ge(exped.sem, exped.at(u, t + 1))
                nc.vector.tensor_reduce(sm[:, t, :, :], prob[t][:, :, :, :], AX.X, ALU.add).then_inc(sumd.sem, 1)
                dve.wait_ge(sumd.sem, sumd.at(u, t + 1))
                nc.vector.reciprocal(rs[:, t, :, :], sm[:, t, :, :]).then_inc(inved.sem, 1)

            def normalise(u, t, a):
                dve.wait_ge(pv.sem, pv.at(u, 2 * t + a + 1))
                dve.wait_ge(inved.sem, inved.at(u, t + 1))
                if a == 0:
                    dve.wait_ge(p_turned.sem, p_turned.at(u, 2 * t + 2))
                src = Bk[a][:, :].rearrange("p (g d) -> p g d", d=DH)
                nc.vector.tensor_tensor(prob[t][:, :, a, :], src, rs[:, t, :, a].unsqueeze(2).broadcast_to([P, G, DH]),
                                        ALU.mult).then_inc(o_kept.sem, 1)

            def add_attention(u, j):
                dve.wait_ge(wo_done.sem, wo_done.at(u, 1))
                dve.wait_ge(fin.sem, fin.at(u, 0))
                dve.wait_ge(lna.sem, lna.at(u, 0))
                nc.vector.tensor_tensor(xs[U1, 0:T], E[U1, 0:T], XT[U1, j, 0:T], ALU.add).then_inc(x1_made.sem, 1)
                nc.vector.tensor_tensor(xs[L1, 1:1 + T], E[L1, 0:T], XT[L1, j, 1:1 + T], ALU.add).then_inc(x1_made.sem, 1)

            def ln_stats(u):
                dve.wait_ge(lna.sem, lna.at(u, 1))
                dve.wait_ge(lnb.sem, lnb.at(u, 0))
                c3.begin(u)
                for t in range(NT):
                    ins = nc.vector.bn_stats(st[:, t, :], E[:, t * P:(t + 1) * P])
                c3.link(dve, ins)
                c3.apart(dve)
                for t in range(NT):
                    ins = nc.vector.bn_aggr(mv[:, t, :], st[:, t, :])
                c3.link(dve, ins)
                y, x, tmp = rv[:, :, 0], mv[:, :, 1], rt[:, :, 0]
                rsqrt(nc, dve, c3, y, x, tmp, rv[:, :, 0].bitcast(I32), mv[:, :, 1].bitcast(I32), 0.0, EPS)
                for t in range(NT):
                    nc.vector.tensor_scalar(xn[:, t, :], E[:, t * P:(t + 1) * P], mv[:, t, 0:1], rv[:, t, 0:1],
                                            ALU.subtract, ALU.mult).then_inc(xn_made.sem, 1)

            def gate(u, k):
                m = FK[k][1]
                dve.wait_ge(gated.sem, gated.at(u, k + 1))
                dve.wait_ge(w2_done.sem, w2_done.at(u, 0))
                nc.vector.scalar_tensor_tensor(act_[0:m, k, :], HB[k][0:m, 0:T], par_b1[0:m, 0, k:k + 1], act_[0:m, k, :],
                                               ALU.add, ALU.mult).then_inc(hact.sem, 1)

            def layer_out(u, j):
                dve.wait_ge(w2_done.sem, w2_done.at(u, 1))
                dve.wait_ge(x1_made.sem, x1_made.at(u, 2))
                nc.vector.scalar_tensor_tensor(XT[U1, j, 0:T], E[U1, 0:T], par_b2[U1, 0:1], xs[U1, 0:T],
                                               ALU.add, ALU.add).then_inc(fin.sem, 1)
                nc.vector.scalar_tensor_tensor(XT[L1, j, 1:1 + T], E[L1, 0:T], par_b2[L1, 0:1], xs[L1, 1:1 + T],
                                               ALU.add, ALU.add).then_inc(fin.sem, 1)

            def body(i, j, p, on, layer0, new, ffn):
                s1, s2, s3 = on
                a, b, q = i - 1, i - 2, 1 - p
                jb = j + 6 if isinstance(j, int) and j < 2 else j - 2
                if s1:
                    x_lo(i, j)
                    rotate(i, 0)
                    rotate(i, 1)
                if new is not None:
                    for c in range(STAGE, NCH):
                        split_chunk(new, c)
                if s2:
                    row_max(a, 0, 0)
                    row_max(a, 0, 1)
                    take_max(a, 0, 0)
                    take_max(a, 0, 1)
                if s1:
                    rotate(i, 2)
                if s3:
                    normalise(b, 1, 0)
                    normalise(b, 1, 1)
                if s1:
                    rotate(i, 3)
                if s2:
                    row_sum(a, 0)
                if s3:
                    add_attention(b, jb)
                    ln_stats(b)
                if s1:
                    rotate(i, 6)
                if s2:
                    row_max(a, 1, 0)
                    row_max(a, 1, 1)
                    take_max(a, 1, 0)
                    take_max(a, 1, 1)
                if s1:
                    rotate(i, 7)
                if s2:
                    normalise(a, 0, 0)
                    normalise(a, 0, 1)
                if s3:
                    gate(b, 0)
                    gate(b, 1)
                if s1:
                    rotate(i, 8)
                    rotate(i, 9)
                if s3:
                    gate(b, 2)
                if s2:
                    row_sum(a, 1)
                if s3:
                    layer_out(b, jb)
            units(dve, body, split_weights)


def overlapped(eng, prepare, first, second):
    prepare(0, 0, 0)
    first(0, 0)
    prepare(1, 1, 0)
    second(0, 0)
    with eng.Fori(1, B // 2) as m:
        first(m * 2 - 1, 1)
        prepare(m * 2, 0, m)
        second(m * 2 - 1, 1)
        first(m * 2, 0)
        prepare(m * 2 + 1, 1, m)
        second(m * 2, 0)
    first(B - 1, 1)
    second(B - 1, 1)


def column(v):
    return v.rearrange("(p a) -> p a", a=1)


def load_constants(nc, bufs, bank, sem, ap):
    ident, identb, wa, wb, wc, wsrc, wtgt, wout = (bufs[k] for k in "ident identb wa wb wc wsrc wtgt wout".split())
    cols, loaded, made, turned, kept = bufs["cols"], sem("c_loaded"), sem("c_made"), sem("c_turned"), sem("c_kept")
    loads = [(wa["raw"], ap["Wa_w"]), (wb["raw"], ap["WB_w"]), (wc["raw"], ap["WC_w"]),
             (wsrc["raw"], ap["W_src"].rearrange("(a p) f -> p a f", p=P)), (wtgt["raw"], ap["W_tgt"]),
             (wout["raw"], ap["W_out"])]
    loads += cols
    with nc.Block() as block:

        @block.sync
        def _(sp):
            for dst, src in loads:
                sp.dma_start(dst, src, allow_slow_non_contiguous=True).then_inc(loaded, 16)
            sp.wait_ge(loaded, 16 * len(loads))

        @block.gpsimd
        def _(pool):
            nc.gpsimd.memset(ident, 0.0).then_inc(made, 1)
            pool.wait_ge(made, 1)
            nc.gpsimd.affine_select(out=ident, in_=ident, compare_op=ALU.not_equal, fill=1.0, base=0,
                                    pattern=[[-1, P]], channel_multiplier=1).then_inc(made, 1)
            pool.wait_ge(made, 2)
            nc.gpsimd.memset(bufs["zero_col"], 0.0).then_inc(made, 1)
            pool.wait_ge(made, 3)
            nc.gpsimd.memset(bufs["v_pad"], 0.0).then_inc(made, 1)
            pool.wait_ge(made, 4)
            nc.gpsimd.memset(bufs["minus_two"], -2.0).then_inc(made, 1)

        @block.tensor
        def _(pe):
            pe.wait_ge(loaded, 16 * len(loads))
            pe.wait_ge(made, 2)
            nc.tensor.transpose(bank[0][:, 0:ST], wa["raw"], ident[0:ST, 0:ST])
            nc.tensor.transpose(bank[0][:, ST:2 * ST], wb["raw"], ident[0:ST, 0:ST])
            nc.tensor.transpose(bank[0][:, P:2 * P], wtgt["raw"], ident)
            for f in range(2):
                nc.tensor.transpose(bank[0][:, (2 + f) * P:(3 + f) * P], wout["raw"][:, f * P:(f + 1) * P], ident)
            for f in range(2):
                for a in range(2):
                    nc.tensor.transpose(bank[1][:, (2 * f + a) * P:(2 * f + a + 1) * P], wsrc["raw"][:, a, f * P:(f + 1) * P], ident)
            nc.tensor.transpose(bank[2][0:ST, 0:P], wc["raw"], ident).then_inc(turned, 1)

        @block.vector
        def _(dve):
            dve.wait_ge(turned, 1)
            nc.vector.tensor_copy(wa["t"], bank[0][:, 0:ST])
            nc.vector.tensor_copy(wb["t"], bank[0][:, ST:2 * ST])
            nc.vector.tensor_copy(wtgt["t"], bank[0][:, P:2 * P])
            nc.vector.tensor_copy(wout["t"], bank[0][:, 2 * P:].rearrange("p (f o) -> p f o", o=P))
            nc.vector.tensor_copy(wsrc["t"], bank[1][:, :].rearrange("p (f o) -> p f o", o=2 * P))
            nc.vector.tensor_copy(wc["t"], bank[2][0:ST, 0:P])
            dve.wait_ge(made, 2)
            nc.vector.tensor_copy(identb, ident).then_inc(kept, 1)


def recurrence_inputs(nc, sb, sem, ap, bank, bufs, XR, XI, aS, uS):
    ident = bufs["ident"]
    N = B * NT
    xt, xi, xn = sb("x_tok", [P, N, D]), sb("xin_tok", [P, N, D]), sb("xn_tok", [P, N, D])
    xnT = [sb(f"xnT_{z}", [P, T]) for z in range(2)]
    st, mv, rv, rt = sb("st1", [P, N, 6]), sb("mv1", [P, N, 2]), sb("rv1", [P, N]), sb("rt1", [P, N])
    loaded = [sem(f"x_loaded{b}") for b in range(B)]
    chain = Chain(sem("chain_in"), 0, bufs["passed"])
    normed = sem("xin_normed"), sem("xn_normed")
    turned = Count(sem("x_turned"), 2)
    kept = Count(sem("xT_kept"), 3)
    proj = Count(sem("au_done"), 1)
    au = Count(sem("au_kept"), 2)

    with nc.Block() as block:

        @block.sync
        def _(sp):
            for b in range(B):
                sp.dma_start(xt[:, b * NT:(b + 1) * NT, :], ap["x"][b].rearrange("(t p) d -> p t d", p=P)).then_inc(loaded[b], 16)

        @block.vector
        def _(dve):
            chain.begin(0)
            for src, dst, done in ((xt, xi, normed[0]), (xi, xn, normed[1])):
                for n in range(N):
                    if done is normed[0]:
                        dve.wait_ge(loaded[n // NT], 16)
                    else:
                        dve.wait_ge(normed[0], n + 1)
                    ins = nc.vector.bn_stats(st[:, n, :], src[:, n, :])
                chain.link(dve, ins)
                for n in range(N):
                    ins = nc.vector.bn_aggr(mv[:, n, :], st[:, n, :])
                chain.link(dve, ins)
                rsqrt(nc, dve, chain, rv[:, :], mv[:, :, 1], rt[:, :], rv[:, :].bitcast(I32), mv[:, :, 1].bitcast(I32), 0.0, EPS)
                for n in range(N):
                    nc.vector.tensor_scalar(dst[:, n, :], src[:, n, :], mv[:, n, 0:1], rv[:, n:n + 1],
                                            ALU.subtract, ALU.mult).then_inc(done, 1)

        @block.tensor
        def _(pe):
            for b in range(B):
                z = b % 2
                pe.wait_ge(normed[0], b * NT + NT)
                if b >= 2:
                    pe.wait_ge(kept.sem, kept.at(b - 2, 3))
                for t in range(NT):
                    nc.tensor.transpose(bank[z][:, t * P:(t + 1) * P], xt[:, b * NT + t, :], ident)
                for t in range(NT):
                    mm = nc.tensor.transpose(bank[z][:, T + t * P:T + (t + 1) * P], xi[:, b * NT + t, :], ident)
                mm.then_inc(turned.sem, 1)
                pe.wait_ge(normed[1], b * NT + NT)
                for t in range(NT):
                    mm = nc.tensor.transpose(bank[2 + z][:, t * P:(t + 1) * P], xn[:, b * NT + t, :], ident)
                mm.then_inc(turned.sem, 1)
                q = b % QUAD * ST
                pe.wait_ge(kept.sem, kept.at(b, 3))
                if b >= 2:
                    pe.wait_ge(au.sem, au.at(b - 2, 2))
                nc.tensor.matmul(bank[4 + z][q:q + ST, 0:T], bufs["wa"]["t"], xnT[z][:, :], start=True, stop=True)
                nc.tensor.matmul(bank[4 + z][q:q + ST, T:2 * T], bufs["wb"]["t"], xnT[z][:, :], start=True, stop=True).then_inc(proj.sem, 1)

        @block.scalar
        def _(act):
            for b in range(B):
                z = b % 2
                act.wait_ge(turned.sem, turned.at(b, 1))
                nc.scalar.activation(XR[:, b, :], bank[z][:, 0:T], ACT.Copy).then_inc(kept.sem, 1)
                nc.scalar.activation(XI[:, b, :], bank[z][:, T:2 * T], ACT.Copy).then_inc(kept.sem, 1)
                act.wait_ge(turned.sem, turned.at(b, 2))
                if b >= 2:
                    act.wait_ge(proj.sem, proj.at(b - 2, 1))
                nc.scalar.activation(xnT[z][:, :], bank[2 + z][:, 0:T], ACT.Identity, scale=bufs["ln_w1"], bias=bufs["ln_b1"]).then_inc(kept.sem, 1)
                act.wait_ge(proj.sem, proj.at(b, 1))
                q = slice(b % QUAD * ST, (b % QUAD + 1) * ST)
                nc.scalar.activation(aS[q, b // QUAD, :], bank[4 + z][q, 0:T], ACT.Tanh, bias=bufs["Wa_b"][q, :]).then_inc(au.sem, 1)
                nc.scalar.activation(uS[q, b // QUAD, :], bank[4 + z][q, T:2 * T], ACT.Identity, bias=bufs["WB_b"][q, :]).then_inc(au.sem, 1)


def recurrence(nc, sb, sem, ap, bank, bufs, XR, XI, aS, uS):
    R2 = 2 * B
    NQ = B // QUAD
    fre, fim, frr = sb("dft_re", [P, NQ, P]), sb("dft_im", [P, NQ, P]), sb("dft_real", [P, NQ, R2])
    gre, gim, grr = sb("idft_re", [P, B, ST]), sb("idft_im", [P, B, ST]), sb("idft_real", [R2, B, ST])
    M = sb("a_u_planes", [P, 4, T])
    R = sb("a_u_real", [R2, 2, T])
    HR = sb("h_real", [R2, T])
    sqm = sb("sq_mag", [P, 2, T])
    mag = sb("mag", [P, T])
    gate = sb("gate", [P, T])
    mag_r, gate_r = sb("mag_r", [R2, T]), sb("gate_r", [R2, T])
    t1, t2 = sb("scan_t1", [P, 4, T]), sb("scan_t2", [P, 4, T])
    hT = sb("hT", [ST, B * T])
    gam = sb("gamma", [P, 1])
    loaded, chain, achain = sem("dft_loaded"), Chain(sem("chain_scan")), Chain(sem("chain_gate_act"))
    gdone, dft, hs, inv, hk, yd = sem("gamma_done"), sem("dft_done"), sem("h_done"), sem("idft_done"), sem("hT_kept"), sem("y_done")
    XRf, XIf = XR.rearrange("p b t -> p (b t)"), XI.rearrange("p b t -> p (b t)")
    LEVELS = [1 << k for k in range(T.bit_length() - 1)]
    tabs = [(fre, "c_dft_re"), (fim, "c_dft_im"), (frr, "c_dft_real"), (gre, "c_idft_re"), (gim, "c_idft_im"), (grr, "c_idft_real")]

    with nc.Block() as block:

        @block.sync
        def _(sp):
            for dst, name in tabs:
                sp.dma_start(dst[tuple([slice(None)] * len(dst.shape))], ap[name]).then_inc(loaded, 16)

        @block.scalar
        def _(act):
            nc.scalar.activation(gam[:, :], bufs["log_gamma"], ACT.Exp, scale=-1.0).then_inc(gdone, 1)
            act.wait_ge(dft, 1)
            achain.begin(0)
            nc.scalar.activation(sqm[:, :, :], bank[0][:, :].rearrange("p (a t) -> p a t", a=2), ACT.Square).then_inc(achain.sem, 1)
            nc.scalar.activation(mag_r[:, :], bank[2][0:R2, 0:T], ACT.Square).then_inc(achain.sem, 1)
            nc.scalar.activation(M[:, 2:4, :], bank[1][:, :].rearrange("p (a t) -> p a t", a=2), ACT.Copy).then_inc(achain.sem, 1)
            nc.scalar.activation(R[:, 1, :], bank[2][0:R2, T:2 * T], ACT.Copy).then_inc(achain.sem, 1)
            act.wait_ge(chain.sem, 5)
            nc.scalar.activation(mag[:, :], mag[:, :], ACT.Sqrt).then_inc(achain.sem, 1)
            nc.scalar.activation(mag_r[:, :], mag_r[:, :], ACT.Sqrt).then_inc(achain.sem, 1)
            act.wait_ge(achain.sem, 6)
            nc.scalar.activation(gate[:, :], mag[:, :], ACT.Exp, scale=2.0, bias=bufs["minus_two"]).then_inc(achain.sem, 1)
            nc.scalar.activation(gate_r[:, :], mag_r[:, :], ACT.Exp, scale=2.0, bias=bufs["minus_two"][0:R2, :]).then_inc(achain.sem, 1)
            for c in range(4):
                act.wait_ge(inv, c + 1)
                nc.scalar.activation(hT[:, c * CH:(c + 1) * CH], bank[3 + c][0:ST, :], ACT.Copy).then_inc(hk, 1)

        @block.tensor
        def _(pe):
            pe.wait_ge(loaded, 16 * len(tabs))
            pe.wait_ge(gdone, 2)
            for o, f, src in ((bank[0][:, 0:T], fre, aS), (bank[0][:, T:2 * T], fim, aS), (bank[1][:, 0:T], fre, uS),
                              (bank[1][:, T:2 * T], fim, uS), (bank[2][0:R2, 0:T], frr, aS), (bank[2][0:R2, T:2 * T], frr, uS)):
                for g in range(NQ):
                    mm = nc.tensor.matmul(o, f[:, g, :], src[:, g, :], start=(g == 0), stop=(g == NQ - 1))
            mm.then_inc(dft, 1)
            pe.wait_ge(hs, 2)
            for b in range(B):
                o = bank[3 + b // 2][0:ST, (b % 2) * T:(b % 2 + 1) * T]
                nc.tensor.matmul(o, gre[:, b, :], M[:, 2, :], start=True, stop=False)
                nc.tensor.matmul(o, gim[:, b, :], M[:, 3, :], start=False, stop=False)
                mm = nc.tensor.matmul(o, grr[:, b, :], HR[:, :], start=False, stop=True)
                if b % 2:
                    mm.then_inc(inv, 1)
            for c in range(4):
                pe.wait_ge(hk, c + 1)
                nc.tensor.matmul(bank[c][:, :] if c < 3 else bank[7][:, :], bufs["wc"]["t"], hT[:, c * CH:(c + 1) * CH],
                                 start=True, stop=True).then_inc(yd, 1)

        @block.vector
        def _(dve):
            dve.wait_ge(gdone, 1)
            chain.begin(0)
            chain.link(dve, nc.vector.tensor_scalar(gam[:, :], gam[:, :], 1.0, None, ALU.add))
            chain.link(dve, nc.vector.reciprocal(gam[:, :], gam[:, :]))
            nc.vector.tensor_scalar(aS, aS, gam[:, 0:1], None, ALU.mult).then_inc(gdone, 1)
            dve.wait_ge(achain.sem, 2)
            chain.link(dve, nc.vector.tensor_tensor(mag[:, :], sqm[:, 0, :], sqm[:, 1, :], ALU.add))
            chain.link(dve, nc.vector.tensor_scalar(mag[:, :], mag[:, :], 1e-16, None, ALU.max))
            chain.link(dve, nc.vector.tensor_scalar(mag_r[:, :], mag_r[:, :], 1e-16, None, ALU.max))
            dve.wait_ge(achain.sem, 8)
            for g_ in (gate, gate_r):
                chain.link(dve, nc.vector.tensor_scalar(g_[:, :], g_[:, :], 1.0, None, ALU.add))
                chain.link(dve, nc.vector.reciprocal(g_[:, :], g_[:, :]))
            chain.link(dve, nc.vector.tensor_tensor(M[:, 0:2, :], bank[0][:, :].rearrange("p (a t) -> p a t", a=2),
                                                    gate[:, :].unsqueeze(1).broadcast_to([P, 2, T]), ALU.mult))
            chain.link(dve, nc.vector.tensor_tensor(R[:, 0, :], bank[2][0:R2, 0:T], gate_r[:, :], ALU.mult))
            nc.vector.tensor_tensor_scan(HR[:, :], R[:, 0, :], R[:, 1, :], 0.0, ALU.mult, ALU.add).then_inc(hs, 1)
            for d in LEVELS:
                last = d == LEVELS[-1]
                pl = slice(2, 4) if last else slice(0, 4)
                np_, n = (2, T - d) if last else (4, T - d)
                for tt, plane in ((t1, 0), (t2, 1)):
                    chain.link(dve, nc.vector.tensor_tensor(tt[:, pl, 0:n], M[:, pl, 0:n],
                                                            M[:, plane, d:].unsqueeze(1).broadcast_to([P, np_, n]), ALU.mult))
                if not last:
                    chain.link(dve, nc.vector.tensor_tensor(M[:, 0, d:], t1[:, 0, 0:n], t2[:, 1, 0:n], ALU.subtract))
                    chain.link(dve, nc.vector.tensor_tensor(M[:, 1, d:], t1[:, 1, 0:n], t2[:, 0, 0:n], ALU.add))
                chain.link(dve, nc.vector.tensor_tensor(t1[:, 2, 0:n], t1[:, 2, 0:n], t2[:, 3, 0:n], ALU.subtract))
                chain.link(dve, nc.vector.tensor_tensor(t1[:, 3, 0:n], t1[:, 3, 0:n], t2[:, 2, 0:n], ALU.add))
                chain.link(dve, nc.vector.tensor_tensor(M[:, 2:4, d:], M[:, 2:4, d:], t1[:, 2:4, 0:n], ALU.add))
            nc.vector.tensor_copy(gam[:, :], gam[:, :]).then_inc(hs, 1)
            for c in range(4):
                x = XRf[:, c * CH:(c + 1) * CH]
                dve.wait_ge(yd, c + 1)
                chain.link(dve, nc.vector.scalar_tensor_tensor(x, (bank[c] if c < 3 else bank[7])[:, :], bufs["WC_b"], x, ALU.add, ALU.add))
                chain.link(dve, nc.vector.scalar_tensor_tensor(x, XIf[:, c * CH:(c + 1) * CH], bufs["D_skip"], x, ALU.mult, ALU.add))


def norm_batches(nc, sb, sem, bank, bufs, tag, src, keep):
    N = B * NT
    PER = CH // P
    ident = bufs["ident"]
    tok = sb(f"tok_{tag}", [P, N, D])
    st, mv, rv, rt = (sb(f"{n}_{tag}", [P, N] + k) for n, k in (("st", [6]), ("mv", [2]), ("rv", []), ("rt", [])))
    there, normed, back, kept = (sem(f"{n}_{tag}") for n in ("turned", "normed", "turned_back", "kept"))
    chain = Chain(sem(f"chain_{tag}"), 0, bufs["passed"])

    def tile_of(n):
        return n // PER, slice(n % PER * P, (n % PER + 1) * P)

    with nc.Block() as block:

        @block.tensor
        def _(pe):
            for n in range(N):
                c, cols = tile_of(n)
                mm = nc.tensor.transpose(bank[c][:, cols], src[:, n // NT, n % NT * P:(n % NT + 1) * P], ident)
                if n % PER == PER - 1:
                    mm.then_inc(there, 1)
            for n in range(N):
                c, cols = tile_of(n)
                pe.wait_ge(normed, n + 1)
                mm = nc.tensor.transpose(bank[4 + c][:, cols], tok[:, n, :], ident)
                if n % PER == PER - 1:
                    mm.then_inc(back, 1)

        @block.vector
        def _(dve):
            chain.begin(0)
            for n in range(N):
                c, cols = tile_of(n)
                dve.wait_ge(there, c + 1)
                ins = nc.vector.bn_stats(st[:, n, :], bank[c][:, cols])
            chain.link(dve, ins)
            for n in range(N):
                ins = nc.vector.bn_aggr(mv[:, n, :], st[:, n, :])
            chain.link(dve, ins)
            rsqrt(nc, dve, chain, rv[:, :], mv[:, :, 1], rt[:, :], rv[:, :].bitcast(I32), mv[:, :, 1].bitcast(I32), 0.0, EPS)
            for n in range(N):
                c, cols = tile_of(n)
                nc.vector.tensor_scalar(tok[:, n, :], bank[c][:, cols], mv[:, n, 0:1], rv[:, n:n + 1],
                                        ALU.subtract, ALU.mult).then_inc(normed, 1)

        @block.scalar
        def _(act):
            for c in range(N // PER):
                act.wait_ge(back, c + 1)
                keep(c, bank[4 + c][:, :].rearrange("p (b t) -> p b t", t=T), kept)


def cross_attention(nc, sb, sem, ap, bank, bufs, XR, TG):
    ident, identb = bufs["ident"], bufs["identb"]
    ctx = [sb(f"ctx_tok{z}", [P, NT, CF]) for z in range(2)]
    mrow = [sb(f"mask_rows{z}", [P, S]) for z in range(2)]
    mcol = [sb(f"mask_cols{z}", [P, NT]) for z in range(2)]
    cT = sb("ctxT", [P, 2, S])
    q = sb("q_x", [P, T])
    k = sb("k_x", [P, S])
    kh = sb("k_heads", [P, XH, S])
    mb = sb("mask_bias", [P, S], BF16)
    v = sb("v_x", [P, NT, D])
    vp = [bufs["v_pad"][:, z, :, :, :] for z in range(2)]
    pr = [sb(f"pr{t}", [P, XH, S]) for t in range(NT)]
    mx, nm, sm = sb("mx_x", [P, NT, XH]), sb("nm_x", [P, NT, XH]), sb("sm_x", [P, NT, XH])
    pT = [sb(f"prT{t}", [P, XH, 2, P]) for t in range(NT)]
    up = sb("updT", [P, T])
    sc, pt, pvb, ms = bank[0:4], bank[4:6], bank[6], bank[7]
    c_loaded = [Count(sem(f"ctx_loaded{z}"), 16 * 4) for z in range(2)]
    pe_ms = Count(sem("inputs_projected"), 4)
    wout_done = Count(sem("wout_done"), 1)
    x3_made = Count(sem("x3_made"), 1)
    chain = Chain(sem("chain_x"), 0, bufs["passed"])
    a_ms = Count(sem("ctxT_kept"), 1)
    v_ms = Count(sem("inputs_kept"), 3)
    scd = Count(sem("scores_x"), 8)
    mxd = Count(sem("max_x"), 8)
    exd = Count(sem("exp_x"), 8 * 2)
    nmd = Count(sem("norm_x"), 2)
    ptd = Count(sem("probs_turned_x"), 8)
    ptk = Count(sem("probT_kept_x"), 8)
    pvd = Count(sem("pv_x"), 2)
    upk = Count(sem("upd_kept"), 2)
    CH_OPS = 13
    chain.per = CH_OPS

    with nc.Block() as block:

        @block.sync
        def _(sp):
            def load(b, z):
                s = c_loaded[z].sem
                sp.dma_start(ctx[z][:, :, :], ap["ctx"][b].rearrange("(t p) f -> p t f", p=P)).then_inc(s, 16)
                m = ap["mask"][b]
                sp.dma_start(mrow[z][:, :], m.rearrange("(a n) -> a n", a=1).broadcast_to([P, S])).then_inc(s, 16)
                for t in range(NT):
                    sp.dma_start(mcol[z][:, t:t + 1], column(m[t * P:(t + 1) * P]), allow_slow_non_contiguous=True).then_inc(s, 16)
            for z in range(2):
                load(z, z)
            with sp.Fori(1, B // 2) as m:
                for z in range(2):
                    sp.wait_ge(v_ms.sem, v_ms.at(m * 2 + z - 2, 3))
                    load(m * 2 + z, z)

        @block.tensor
        def _(pe):
            def prepare(b, z, m):
                pe.wait_ge(c_loaded[z].sem, c_loaded[z].at(m, 64))
                pe.wait_ge(exd.sem, exd.at(b, 0))
                for f in range(2):
                    for t in range(NT):
                        mm = nc.tensor.transpose(sc[0][:, f * S + t * P:f * S + (t + 1) * P], ctx[z][:, t, f * P:(f + 1) * P], ident)
                mm.then_inc(pe_ms.sem, 1)
                pe.wait_ge(a_ms.sem, a_ms.at(b, 1))
                for f in range(2):
                    mm = nc.tensor.matmul(sc[1][:, 0:S], bufs["wsrc"]["t"][:, f, 0:P], cT[:, f, :], start=(f == 0), stop=(f == 1))
                mm.then_inc(pe_ms.sem, 1)
                for t in range(NT):
                    for f in range(2):
                        mm = nc.tensor.matmul(sc[2][:, t * P:(t + 1) * P], cT[:, f, t * P:(t + 1) * P],
                                              bufs["wsrc"]["t"][:, f, P:2 * P], start=(f == 0), stop=(f == 1))
                mm.then_inc(pe_ms.sem, 1)
                nc.tensor.matmul(sc[3][:, 0:T], bufs["wtgt"]["t"], TG[:, b, :], start=True, stop=True).then_inc(pe_ms.sem, 1)

            def turn_probs(b, t):
                pe.wait_ge(nmd.sem, nmd.at(b, t + 1))
                for h in range(4):
                    pe.wait_ge(ptk.sem, ptk.at(b, max(4 * t + h - 1, 0)))
                    for a in range(2):
                        for s in range(2):
                            mm = nc.tensor.transpose(pt[h % 2][:, (2 * a + s) * P:(2 * a + s + 1) * P],
                                                     pr[t][:, 2 * h + a, s * P:(s + 1) * P], ident)
                    mm.then_inc(ptd.sem, 1)

            def update(b, z, t):
                pe.wait_ge(ptk.sem, ptk.at(b, 4 * t + 4))
                if t == 0:
                    pe.wait_ge(upk.sem, upk.at(b, 0))
                for a in range(2):
                    for s in range(2):
                        for j in range(4):
                            mm = nc.tensor.matmul(pvb[32 * j:32 * j + 32, t * P:(t + 1) * P], vp[z][:, s, a, 32 * j:32 * j + 32],
                                                  pT[t][:, 2 * j + a, s, :], start=(a == 0 and s == 0), stop=(a == 1 and s == 1),
                                                  skip_group_check=True)
                mm.then_inc(pvd.sem, 1)

            def first(b, z):
                for t in range(NT):
                    for h in range(4):
                        if t == 0 and h == 0:
                            pe.wait_ge(v_ms.sem, v_ms.at(b, 3))
                        if t == 1:
                            pe.wait_ge(exd.sem, exd.at(b, 2 * h + 2))
                        nc.tensor.matmul(sc[h][:, :], identb, mb[:, :].unsqueeze(1).broadcast_to([P, 2, S]), start=True, stop=False)
                        nc.tensor.matmul(sc[h][:, :], q[:, t * P:(t + 1) * P], kh[:, 2 * h:2 * h + 2, :].rearrange("p h s -> p (h s)"),
                                         start=False, stop=True).then_inc(scd.sem, 1)
                turn_probs(b, 0)

            def second(b, z):
                update(b, z, 0)
                turn_probs(b, 1)
                update(b, z, 1)
                pe.wait_ge(upk.sem, upk.at(b, 2))
                pe.wait_ge(x3_made.sem, x3_made.at(b, 0))
                nc.tensor.matmul(ms[:, 0:T], bufs["wout"]["t"][:, 0, :], TG[:, b, :], start=True, stop=False)
                nc.tensor.matmul(ms[:, 0:T], bufs["wout"]["t"][:, 1, :], up[:, :], start=False, stop=True).then_inc(wout_done.sem, 1)
            overlapped(pe, prepare, first, second)

        @block.scalar
        def _(act):
            def prepare(b, z, m):
                act.wait_ge(pe_ms.sem, pe_ms.at(b, 1))
                nc.scalar.activation(cT[:, :, :], sc[0][:, :].rearrange("p (f s) -> p f s", f=2), ACT.Copy).then_inc(a_ms.sem, 1)

            def keep_probs(b, t):
                for h in range(4):
                    act.wait_ge(ptd.sem, ptd.at(b, 4 * t + h + 1))
                    nc.scalar.activation(pT[t][:, 2 * h:2 * h + 2, :, :], pt[h % 2][:, :].rearrange("p (h s t) -> p h s t", h=2, s=2),
                                         ACT.Copy).then_inc(ptk.sem, 1)

            def keep_update(b, t):
                act.wait_ge(pvd.sem, pvd.at(b, t + 1))
                nc.scalar.activation(up[:, t * P:(t + 1) * P], pvb[:, t * P:(t + 1) * P], ACT.Copy).then_inc(upk.sem, 1)

            def first(b, z):
                for t in range(NT):
                    for h in range(4):
                        act.wait_ge(mxd.sem, mxd.at(b, 4 * t + h + 1))
                        for a in range(2):
                            n = 2 * h + a
                            nc.scalar.activation(pr[t][:, n, :], sc[h][:, a * S:(a + 1) * S], ACT.Exp, bias=nm[:, t, n:n + 1],
                                                 scale=float(XD) ** -0.5, accum_out=sm[:, t, n:n + 1]).then_inc(exd.sem, 1)
                keep_probs(b, 0)

            def second(b, z):
                keep_update(b, 0)
                keep_probs(b, 1)
                keep_update(b, 1)
            overlapped(act, prepare, first, second)

        @block.vector
        def _(dve):
            link = lambda ins: chain.link(dve, ins)

            def prepare(b, z, m):
                chain.begin(b)
                dve.wait_ge(c_loaded[z].sem, c_loaded[z].at(m, 64))
                dve.wait_ge(scd.sem, scd.at(b, 0))
                link(nc.vector.tensor_scalar(mb[:, :], mrow[z][:, :], 0.0, NEG, ALU.is_equal, ALU.mult))
                dve.wait_ge(pe_ms.sem, pe_ms.at(b, 2))
                link(nc.vector.scalar_tensor_tensor(k[:, :], sc[1][:, 0:S], bufs["b_k"], mrow[z][:, :], ALU.add, ALU.mult))
                for h in range(XH):
                    ins = nc.vector.tensor_scalar(kh[:, h, :], k[:, :], bufs["headmask"][:, h:h + 1], None, ALU.mult)
                ins.then_inc(v_ms.sem, 1)
                dve.wait_ge(pe_ms.sem, pe_ms.at(b, 3))
                link(nc.vector.tensor_tensor(v[:, :, :], sc[2][:, 0:T].rearrange("p (t c) -> p t c", t=NT),
                                             bufs["b_v"].unsqueeze(1).broadcast_to([P, NT, D]), ALU.add))
                for t in range(NT):
                    for a in range(2):
                        ins = nc.vector.tensor_scalar(vp[z][:, t, a, :].rearrange("p (j a d) -> p j a d", a=2, d=XD)[:, :, a, :],
                                                      v[:, t, :].rearrange("p (j a d) -> p j a d", a=2, d=XD)[:, :, a, :],
                                                      mcol[z][:, t:t + 1], None, ALU.mult)
                ins.then_inc(v_ms.sem, 1)
                dve.wait_ge(pe_ms.sem, pe_ms.at(b, 4))
                nc.vector.scalar_tensor_tensor(q[:, :], sc[3][:, 0:T], bufs["b_q"], mrow[z][:, :], ALU.add, ALU.mult).then_inc(v_ms.sem, 1)

            def maxima(b, t, h):
                dve.wait_ge(scd.sem, scd.at(b, 4 * t + h + 1))
                link(nc.vector.tensor_reduce(mx[:, t, 2 * h:2 * h + 2], sc[h][:, :].rearrange("p (a s) -> p a s", a=2), AX.X, ALU.max))
                nc.vector.tensor_scalar(nm[:, t, 2 * h:2 * h + 2], mx[:, t, 2 * h:2 * h + 2], -float(XD) ** -0.5, None,
                                        ALU.mult).then_inc(mxd.sem, 1)

            def normalise(b, t):
                dve.wait_ge(exd.sem, exd.at(b, 8 * t + 8))
                link(nc.vector.reciprocal(sm[:, t, :], sm[:, t, :]))
                for h in range(XH):
                    ins = nc.vector.tensor_scalar(pr[t][:, h, :], pr[t][:, h, :], sm[:, t, h:h + 1], None, ALU.mult)
                ins.then_inc(nmd.sem, 1)

            def first(b, z):
                chain.begin(b)
                chain.n = 3
                for h in range(4):
                    maxima(b, 0, h)
                maxima(b, 1, 0)
                maxima(b, 1, 1)
                normalise(b, 0)
                maxima(b, 1, 2)
                maxima(b, 1, 3)
                normalise(b, 1)
                assert chain.n == chain.per, chain.n

            def second(b, z):
                dve.wait_ge(wout_done.sem, wout_done.at(b, 1))
                nc.vector.scalar_tensor_tensor(XR[:, b, :], ms[:, 0:T], bufs["b_o"], XR[:, b, :], ALU.add, ALU.add).then_inc(x3_made.sem, 1)
            overlapped(dve, prepare, first, second)


def output(nc, sb, sem, bank, ident, XR, XT, out):
    y = sb("y", [P, B, T])
    yo = sb("y_tok", [P, B, NT, D])
    summed, turned, kept, stored = sem("y_summed"), sem("y_turned"), sem("y_kept"), sem("y_stored")
    with nc.Block() as block:

        @block.vector
        def _(dve):
            for b in range(B):
                nc.vector.tensor_tensor(y[KEEP, b, :], XR[KEEP, b, :], XT[KEEP, b, 0:T], ALU.add).then_inc(summed, 1)
                nc.vector.tensor_tensor(y[SHIFT, b, :], XR[SHIFT, b, :], XT[SHIFT, b, 1:1 + T], ALU.add).then_inc(summed, 1)

        @block.tensor
        def _(pe):
            for b in range(B):
                pe.wait_ge(summed, 2 * b + 2)
                for t in range(NT):
                    mm = nc.tensor.transpose(bank[b][:, t * P:(t + 1) * P], y[:, b, t * P:(t + 1) * P], ident)
                mm.then_inc(turned, 1)

        @block.scalar
        def _(act):
            for b in range(B):
                act.wait_ge(turned, b + 1)
                nc.scalar.activation(yo[:, b, :, :], bank[b][:, 0:T].rearrange("p (t d) -> p t d", t=NT), ACT.Copy).then_inc(kept, 1)

        @block.sync
        def _(sp):
            for b in range(B):
                sp.wait_ge(kept, b + 1)
                sp.dma_start(out[b].rearrange("(t p) d -> p t d", p=P), yo[:, b, :, :]).then_inc(stored, 16)
            sp.wait_ge(stored, 16 * B)


def decoder_block(nc, ap, out):
    with ExitStack() as ctx:
        def sb_in(stack):
            return lambda n, s, d=F32: stack.enter_context(nc.sbuf_tensor(n, s, d))

        sb = sb_in(ctx)
        sem = lambda n: ctx.enter_context(nc.semaphore(n))
        bank = [ctx.enter_context(nc.psum_tensor(f"bank{n}", [P, CH], F32)) for n in range(8)]
        XT = sb("x_layers", [P, B, 1 + T])
        XRt = sb("x_res", [P, B, T])
        XR = XRt[:, :, :]
        ident_t = sb("ident", [P, P])
        identb_t = sb("ident_bf", [P, P], BF16)
        passed = sem("waits_passed")
        with ExitStack() as first:
            sf = sb_in(first)
            vec = {n: sf(n + "_col", [r, 1]) for n, r in
                   (("Wa_b", P), ("WB_b", P), ("log_gamma", P), ("ln_w1", P), ("ln_b1", P), ("WC_b", P), ("D_skip", P),
                    ("b_k", P), ("b_q", P), ("b_o", P))}
            src = {"ln_w1": ap["ln_w1"], "ln_b1": ap["ln_b1"], "b_k": ap["b_src"][0:P], "b_q": ap["b_tgt"], "b_o": ap["b_out"]}
            cols = []
            for n, t in vec.items():
                if n == "log_gamma":
                    cols.append((t[:, :], ap[n].rearrange("(a n) -> a n", a=1).broadcast_to([P, 1])))
                elif n in ("Wa_b", "WB_b"):
                    cols += [(t[q * ST:(q + 1) * ST, :], column(ap[n])) for q in range(QUAD)]
                else:
                    cols.append((t[:, :], column(src.get(n, ap.get(n)))))
            bv, hm = sf("b_v", [P, D]), sf("headmask", [P, XH])
            cols.append((bv[:, :], ap["b_src"][P:2 * P].rearrange("(a n) -> a n", a=1).broadcast_to([P, D])))
            cols.append((hm[:, :], ap["c_headmask"]))
            two = sf("minus_two", [P, 1])
            vp = sf("v_pad", [P, 2, NT, 2, D])
            bufs = {n: t[:, :] for n, t in vec.items()}
            bufs |= {"passed": passed, "ident": ident_t[:, :], "identb": identb_t[:, :], "b_v": bv[:, :], "headmask": hm[:, :], "minus_two": two[:, :],
                     "v_pad": vp[:, :, :, :, :], "zero_col": XT[:, :, 0:1], "cols": cols}

            def weight(n, raw, t):
                a, b = sf(n + "_raw", raw), sf(n + "_t", t)
                bufs[n] = {"raw": a[tuple([slice(None)] * len(raw))], "t": b[tuple([slice(None)] * len(t))]}
            weight("wa", [ST, D], [D, ST])
            weight("wb", [ST, D], [D, ST])
            weight("wc", [D, ST], [ST, D])
            weight("wsrc", [P, 2, CF], [P, 2, 2 * D])
            weight("wtgt", [P, D], [P, D])
            weight("wout", [P, 2 * D], [P, 2, D])
            load_constants(nc, bufs, bank, sem, ap)
            with ExitStack() as part:
                XI = sb_in(part)("x_in", [P, B, T])[:, :, :]
                aS, uS = (sb_in(part)(n, [P, B // QUAD, T])[:, :, :] for n in ("a_states", "u_states"))
                with ExitStack() as p2:
                    recurrence_inputs(nc, sb_in(p2), sem, ap, bank, bufs, XR, XI, aS, uS)
                with ExitStack() as p2:
                    recurrence(nc, sb_in(p2), sem, ap, bank, bufs, XR, XI, aS, uS)
            with ExitStack() as part:
                TG = sb_in(part)("tgtT", [P, B, T])

                def keep_tgt(c, src, kept):
                    nc.scalar.activation(TG[:, 2 * c:2 * c + 2, :], src, ACT.Copy).then_inc(kept, 1)

                def keep_layers_x(c, src, kept):
                    nc.scalar.activation(XT[KEEP, 2 * c:2 * c + 2, 0:T], src[KEEP, :, :], ACT.Copy).then_inc(kept, 1)
                    nc.scalar.activation(XT[SHIFT, 2 * c:2 * c + 2, 1:1 + T], src[SHIFT, :, :], ACT.Copy).then_inc(kept, 1)
                with ExitStack() as p2:
                    norm_batches(nc, sb_in(p2), sem, bank, bufs, "tgt", XR, keep_tgt)
                with ExitStack() as p2:
                    cross_attention(nc, sb_in(p2), sem, ap, bank, bufs, XR, TG)
                with ExitStack() as p2:
                    norm_batches(nc, sb_in(p2), sem, bank, bufs, "out", XR, keep_layers_x)
        with ExitStack() as part:
            layer_stage(nc, sb_in(part), bank, ident_t, identb_t, passed, sem, ap, XT)
        with ExitStack() as part:
            output(nc, sb_in(part), sem, bank, ident_t[:, :], XR, XT, out)


_INS = {"x": "x", "ctx": "ctx_2048", "mask": "mask_BxS2_fk1", "Wa_w": "L0_attn_Wa_w", "Wa_b": "L0_attn_Wa_b",
        "log_gamma": "L0_attn_log_gamma", "WB_w": "L0_attn_WB_w", "WB_b": "L0_attn_WB_b", "WC_w": "L0_attn_WC_w",
        "WC_b": "L0_attn_WC_b", "D_skip": "L0_attn_D_skip", "ln_w1": "L0_attn_ln_w", "ln_b1": "L0_attn_ln_b",
        "W_src": "L0_xattn_W_src", "b_src": "L0_xattn_b_src", "W_tgt": "L0_xattn_W_tgt", "b_tgt": "L0_xattn_b_tgt",
        "W_out": "L0_xattn_W_out", "b_out": "L0_xattn_b_out", "Wqkv": "L0_ffn_Wqkv", "q_scale": "L0_ffn_q_scale",
        "k_scale": "L0_ffn_k_scale", "Wo": "L0_ffn_Wo", "ln_g": "L0_ffn_ln_g", "ln_b": "L0_ffn_ln_b", "W1": "L0_ffn_W1",
        "b1": "L0_ffn_b1", "W2": "L0_ffn_W2", "b2": "L0_ffn_b2"}


def _tables():
    import numpy as np

    f = np.float32
    half = np.arange(0, DH, 2) * 1.0
    ang = np.arange(T)[:, None] / 10000.0 ** (half / DH)[None, :]
    scale = ((half + 0.4 * DH) / (1.4 * DH))[None, :] ** ((np.arange(T) - T // 2) / (W // 2))[:, None]
    ang, scale = np.concatenate([ang, ang], -1), np.concatenate([scale, scale], -1)
    sign = np.concatenate([-np.ones(DH // 2), np.ones(DH // 2)])
    rotary = np.stack([np.stack([np.cos(ang) * s, np.sin(ang) * s * sign]) for s in (scale, 1 / scale)])
    n = np.arange(ST)
    turn = 2 * np.pi * np.outer(n, np.arange(SLOT)) / ST
    live = (np.arange(SLOT) > 0) * 1.0
    real = np.stack([np.ones(ST), (-1.0) ** n])
    fwd = np.zeros((2, QUAD, ST, B // QUAD, B, SLOT))
    rfwd = np.zeros((QUAD, ST, B // QUAD, B, 2))
    for b in range(B):
        q, g = b % QUAD, b // QUAD
        fwd[0, q, :, g, b, :] = np.cos(turn) * live
        fwd[1, q, :, g, b, :] = -np.sin(turn) * live
        rfwd[q, :, g, b, :] = real.T
    fwd, rfwd = fwd.reshape(2, P, B // QUAD, P), rfwd.reshape(P, B // QUAD, 2 * B)
    back = np.zeros((2, B, SLOT, B, ST))
    rback = np.zeros((B, 2, B, ST))
    for b in range(B):
        back[0, b, :, b, :] = (np.cos(turn) * live).T * 2 / ST
        back[1, b, :, b, :] = -(np.sin(turn) * live).T * 2 / ST
        rback[b, :, b, :] = real / ST
    back = back.reshape(2, P, B, ST)
    head = (np.arange(P)[:, None] // XD == np.arange(XH)[None, :]) * 1.0
    out = {"rotary": rotary, "c_dft_re": fwd[0], "c_dft_im": fwd[1], "c_dft_real": rfwd, "c_idft_re": back[0],
           "c_idft_im": back[1], "c_idft_real": rback.reshape(2 * B, B, ST), "c_headmask": head}
    return {k: np.ascontiguousarray(v.astype(f)) for k, v in out.items()}


def kernel(**inputs):
    import numpy as _np
    import concourse.bacc as _bacc
    from concourse.bass_utils import run_bass_kernel_spmd as _run

    nc = _bacc.Bacc("TRN2", target_bir_lowering=False, num_devices=1)
    arrays = {name: _np.ascontiguousarray(inputs[full]) for name, full in _INS.items()} | _tables()
    feed = {f"in_{name}_dram": a for name, a in arrays.items()}
    ap = {name: nc.dram_tensor(f"in_{name}_dram", a.shape, F32, kind="ExternalInput").ap() for name, a in arrays.items()}
    out = nc.dram_tensor("out_0_dram", (B, T, D), F32, kind="ExternalOutput").ap()
    decoder_block(nc, ap, out)
    r = _run(nc, [feed], core_ids=[0])
    return r.results[0]["out_0_dram"]
```
